# Optimizing a Trainium2 kernel written in Bass

```python
import numpy as np
import jax
import jax.numpy as jnp

def _softmax(x, axis=-1):
    return jax.nn.softmax(x, axis=axis)

def _gelu(x):
    return jax.nn.gelu(x, approximate=True)

def _silu(x):
    return jax.nn.silu(x)

def _sigmoid(x):
    return jax.nn.sigmoid(x)

def _layernorm(x, axis=-1, eps=1e-05):
    m = jnp.mean(x, axis=axis, keepdims=True)
    v = jnp.var(x, axis=axis, keepdims=True)
    return (x - m) / jnp.sqrt(v + eps)

def _scatter_add(tgt, idx, src, axis=0):
    return tgt.at[idx].add(src)

def _segment_sum(src, seg, n):
    return jax.ops.segment_sum(src, seg, n)
kernel_name = 'mk_adj_preln_d2_adj_r2_c4bb34'

def setup_inputs(seed: int=0):
    np.random.seed(seed)
    _w = jnp.asarray

    def _rec_inputs():
        import jax
        import jax.numpy as jnp
        _gk = jax.random.key(seed)
        x = -0.0002928 + 1 * jax.random.normal(jax.random.fold_in(_gk, 1), (32, 256, 128), jnp.float32)
        _a = jax.random.bernoulli(jax.random.fold_in(_gk, 2), 0.015625, (32, 256, 256))
        _a = jnp.logical_or(_a, jnp.swapaxes(_a, -1, -2))
        _a = jnp.logical_or(_a, jnp.eye(256, dtype=bool))
        adj = _a.astype(jnp.int32)
        _nm = jnp.ones((32, 256), dtype=bool)
        nodemask = jnp.where(_nm, 1.0, 0.0).astype(jnp.float32)
        return (x, adj, nodemask)
    x, adj, nodemask = _rec_inputs()

    def _L0_gnn_setup():
        import jax, jax.numpy as jnp
        import numpy as np
        EPS = 1e-05

        def _layernorm(x, w, b):
            m = jnp.mean(x, axis=-1, keepdims=True)
            v = jnp.mean((x - m) ** 2, axis=-1, keepdims=True)
            return (x - m) * jax.lax.rsqrt(v + EPS) * w + b

        def _swish(x):
            return x * jax.nn.sigmoid(x)
        key = jax.random.key(seed)
        ks = jax.random.split(key, 10)
        B, A, D_IN, D_OUT = (8, 1024, 128, 128)
        s_in = 1.0 / np.sqrt(D_IN)
        s_out = 1.0 / np.sqrt(D_OUT)
        return {'x': jax.random.normal(ks[0], (B, A, D_IN), dtype=jnp.float32), 'connectivity': jax.random.randint(ks[1], (B, A, A), 0, 2, dtype=jnp.int32), 'Wq': jax.random.uniform(ks[2], (D_OUT, D_IN), jnp.float32, -s_in, s_in), 'Wk': jax.random.uniform(ks[3], (D_OUT, D_IN), jnp.float32, -s_in, s_in), 'Wv': jax.random.uniform(ks[4], (D_OUT, D_IN), jnp.float32, -s_in, s_in), 'ln1_w': jnp.ones((D_OUT,), jnp.float32), 'ln1_b': jnp.zeros((D_OUT,), jnp.float32), 'W1': jax.random.uniform(ks[5], (D_OUT, D_OUT), jnp.float32, -s_out, s_out), 'b1': jax.random.uniform(ks[6], (D_OUT,), jnp.float32, -s_out, s_out), 'ln2_w': jnp.ones((D_OUT,), jnp.float32), 'ln2_b': jnp.zeros((D_OUT,), jnp.float32), 'W2': jax.random.uniform(ks[7], (D_OUT, D_OUT), jnp.float32, -s_out, s_out), 'b2': jax.random.uniform(ks[8], (D_OUT,), jnp.float32, -s_out, s_out), 'lnf_w': jnp.ones((D_OUT,), jnp.float32), 'lnf_b': jnp.zeros((D_OUT,), jnp.float32)}
    _L0_gnn_all = _L0_gnn_setup()
    _L0_gnn_in = {k: v for k, v in _L0_gnn_all.items() if k in ('Wq', 'Wk', 'Wv', 'ln1_w', 'ln1_b', 'W1', 'b1', 'ln2_w', 'ln2_b', 'W2', 'b2', 'lnf_w', 'lnf_b')}
    del _L0_gnn_all

    def _L1_gnn_setup():
        import jax, jax.numpy as jnp
        import numpy as np
        D_MODEL = 128
        NUM_REL = 40

        def _direction(x, W, Wg, b, bg, adj, rel_ids):
            h = x @ W.T
            g = h @ Wg.T
            vals = (h[:, :, None, :] + b) * jax.nn.sigmoid(g[:, :, None, :] + bg)
            onehot = (adj[..., None] == rel_ids).astype(h.dtype)
            return jnp.einsum('bnmr,bmrd->bnd', onehot, vals)
        key = jax.random.key(seed)
        ks = jax.random.split(key, 16)
        B, N, d = (2, 256, D_MODEL)
        s = 0.02
        inp = {'node': jax.random.normal(ks[0], (B, N, d), dtype=jnp.float32), 'node_mask': jnp.ones((B, N), dtype=jnp.float32), 'adj_mat': jax.random.randint(ks[1], (B, N, N), 0, 41, dtype=jnp.int32), 'W_fwd': jax.random.normal(ks[2], (d, d), dtype=jnp.float32) * s, 'W_bwd': jax.random.normal(ks[3], (d, d), dtype=jnp.float32) * s, 'W_loop': jax.random.normal(ks[4], (d, d), dtype=jnp.float32) * s, 'Wg_fwd': jax.random.normal(ks[5], (d, d), dtype=jnp.float32) * s, 'Wg_bwd': jax.random.normal(ks[6], (d, d), dtype=jnp.float32) * s, 'Wg_loop': jax.random.normal(ks[7], (d, d), dtype=jnp.float32) * s, 'b_fwd': jax.random.normal(ks[8], (NUM_REL - 1, d), dtype=jnp.float32) * s, 'b_bwd': jax.random.normal(ks[9], (NUM_REL - 1, d), dtype=jnp.float32) * s, 'b_loop': jax.random.normal(ks[10], (1, d), dtype=jnp.float32) * s, 'bg_fwd': jax.random.normal(ks[11], (NUM_REL - 1, d), dtype=jnp.float32) * s, 'bg_bwd': jax.random.normal(ks[12], (NUM_REL - 1, d), dtype=jnp.float32) * s, 'bg_loop': jax.random.normal(ks[13], (1, d), dtype=jnp.float32) * s}
        return inp
    _L1_gnn_all = _L1_gnn_setup()
    _L1_gnn_in = {k: v for k, v in _L1_gnn_all.items() if k in ('W_fwd', 'W_bwd', 'W_loop', 'Wg_fwd', 'Wg_bwd', 'Wg_loop', 'b_fwd', 'b_bwd', 'b_loop', 'bg_fwd', 'bg_bwd', 'bg_loop')}
    del _L1_gnn_all
    return {'x': x, 'adj': adj, 'nodemask': nodemask, 'L0_gnn_Wq': _L0_gnn_in['Wq'], 'L0_gnn_Wk': _L0_gnn_in['Wk'], 'L0_gnn_Wv': _L0_gnn_in['Wv'], 'L0_gnn_ln1_w': _L0_gnn_in['ln1_w'], 'L0_gnn_ln1_b': _L0_gnn_in['ln1_b'], 'L0_gnn_W1': _L0_gnn_in['W1'], 'L0_gnn_b1': _L0_gnn_in['b1'], 'L0_gnn_ln2_w': _L0_gnn_in['ln2_w'], 'L0_gnn_ln2_b': _L0_gnn_in['ln2_b'], 'L0_gnn_W2': _L0_gnn_in['W2'], 'L0_gnn_b2': _L0_gnn_in['b2'], 'L0_gnn_lnf_w': _L0_gnn_in['lnf_w'], 'L0_gnn_lnf_b': _L0_gnn_in['lnf_b'], 'L1_gnn_W_fwd': _L1_gnn_in['W_fwd'], 'L1_gnn_W_bwd': _L1_gnn_in['W_bwd'], 'L1_gnn_W_loop': _L1_gnn_in['W_loop'], 'L1_gnn_Wg_fwd': _L1_gnn_in['Wg_fwd'], 'L1_gnn_Wg_bwd': _L1_gnn_in['Wg_bwd'], 'L1_gnn_Wg_loop': _L1_gnn_in['Wg_loop'], 'L1_gnn_b_fwd': _L1_gnn_in['b_fwd'], 'L1_gnn_b_bwd': _L1_gnn_in['b_bwd'], 'L1_gnn_b_loop': _L1_gnn_in['b_loop'], 'L1_gnn_bg_fwd': _L1_gnn_in['bg_fwd'], 'L1_gnn_bg_bwd': _L1_gnn_in['bg_bwd'], 'L1_gnn_bg_loop': _L1_gnn_in['bg_loop']}

def reference(x, adj, nodemask, L0_gnn_Wq, L0_gnn_Wk, L0_gnn_Wv, L0_gnn_ln1_w, L0_gnn_ln1_b, L0_gnn_W1, L0_gnn_b1, L0_gnn_ln2_w, L0_gnn_ln2_b, L0_gnn_W2, L0_gnn_b2, L0_gnn_lnf_w, L0_gnn_lnf_b, L1_gnn_W_fwd, L1_gnn_W_bwd, L1_gnn_W_loop, L1_gnn_Wg_fwd, L1_gnn_Wg_bwd, L1_gnn_Wg_loop, L1_gnn_b_fwd, L1_gnn_b_bwd, L1_gnn_b_loop, L1_gnn_bg_fwd, L1_gnn_bg_bwd, L1_gnn_bg_loop):
    import jax
    import jax.numpy as jnp

    def _L0_gnn_ref(x, connectivity, Wq, Wk, Wv, ln1_w, ln1_b, W1, b1, ln2_w, ln2_b, W2, b2, lnf_w, lnf_b):
        import jax, jax.numpy as jnp
        import numpy as np
        EPS = 1e-05

        def _layernorm(x, w, b):
            m = jnp.mean(x, axis=-1, keepdims=True)
            v = jnp.mean((x - m) ** 2, axis=-1, keepdims=True)
            return (x - m) * jax.lax.rsqrt(v + EPS) * w + b

        def _swish(x):
            return x * jax.nn.sigmoid(x)
        D_OUT = Wq.shape[0]
        scale = jnp.sqrt(jnp.float32(D_OUT))
        Q = jnp.einsum('bah,oh->bao', x, Wq)
        K = jnp.einsum('bah,oh->bao', x, Wk)
        V = jnp.einsum('bah,oh->bao', x, Wv)
        scores = jnp.einsum('bqd,bkd->bqk', Q, K) / scale
        mask = (connectivity == 0).astype(scores.dtype) * -1000000000.0
        alpha = jax.nn.softmax(scores + mask, axis=-1)
        H = jnp.einsum('bqk,bkd->bqd', alpha, V)
        h = _layernorm(_swish(H), ln1_w, ln1_b)
        h = jnp.einsum('bad,od->bao', h, W1) + b1
        h = _layernorm(_swish(h), ln2_w, ln2_b)
        h = jnp.einsum('bad,od->bao', h, W2) + b2
        return _layernorm(h, lnf_w, lnf_b)

    def _L1_gnn_ref(node, node_mask, adj_mat, W_fwd, W_bwd, W_loop, Wg_fwd, Wg_bwd, Wg_loop, b_fwd, b_bwd, b_loop, bg_fwd, bg_bwd, bg_loop):
        import jax, jax.numpy as jnp
        import numpy as np
        D_MODEL = 128
        NUM_REL = 40

        def _direction(x, W, Wg, b, bg, adj, rel_ids):
            h = x @ W.T
            g = h @ Wg.T
            vals = (h[:, :, None, :] + b) * jax.nn.sigmoid(g[:, :, None, :] + bg)
            onehot = (adj[..., None] == rel_ids).astype(h.dtype)
            return jnp.einsum('bnmr,bmrd->bnd', onehot, vals)
        rels = jnp.arange(2, NUM_REL + 1, dtype=adj_mat.dtype)
        rel1 = jnp.array([1], dtype=adj_mat.dtype)
        adj_t = jnp.swapaxes(adj_mat, -1, -2)
        out = _direction(node, W_fwd, Wg_fwd, b_fwd, bg_fwd, adj_mat, rels)
        out = out + _direction(node, W_bwd, Wg_bwd, b_bwd, bg_bwd, adj_t, rels)
        out = out + _direction(node, W_loop, Wg_loop, b_loop, bg_loop, adj_t, rel1)
        return jax.nn.relu(out)
    h = jnp.maximum(_layernorm(x, axis=-1), 0.0)
    x = x + _L0_gnn_ref(h, adj, L0_gnn_Wq, L0_gnn_Wk, L0_gnn_Wv, L0_gnn_ln1_w, L0_gnn_ln1_b, L0_gnn_W1, L0_gnn_b1, L0_gnn_ln2_w, L0_gnn_ln2_b, L0_gnn_W2, L0_gnn_b2, L0_gnn_lnf_w, L0_gnn_lnf_b)
    h = jnp.maximum(_layernorm(x, axis=-1), 0.0)
    x = x + _L1_gnn_ref(h, nodemask, adj, L1_gnn_W_fwd, L1_gnn_W_bwd, L1_gnn_W_loop, L1_gnn_Wg_fwd, L1_gnn_Wg_bwd, L1_gnn_Wg_loop, L1_gnn_b_fwd, L1_gnn_b_bwd, L1_gnn_b_loop, L1_gnn_bg_fwd, L1_gnn_bg_bwd, L1_gnn_bg_loop)
    return x

_drawn_inputs = setup_inputs


def setup_inputs(seed=0):
    import zlib

    import numpy as np

    out = dict(_drawn_inputs(seed))
    spreads = {'L0_gnn_ln1_w': (1.0, 0.2),
     'L0_gnn_ln1_b': (0.0, 0.1),
     'L0_gnn_ln2_w': (1.0, 0.2),
     'L0_gnn_ln2_b': (0.0, 0.1),
     'L0_gnn_lnf_w': (1.0, 0.2),
     'L0_gnn_lnf_b': (0.0, 0.1)}
    factors = {'L1_gnn_Wg_loop': 8.0, 'L1_gnn_bg_loop': 24.256}
    for name, (base, spread) in spreads.items():
        noise = np.random.default_rng([zlib.crc32(name.encode()), seed]).standard_normal(out[name].shape)
        drawn = base * np.exp(spread * noise) if base else spread * noise
        out[name] = jnp.asarray(drawn.astype(out[name].dtype))
    for name, factor in factors.items():
        out[name] = (out[name] * factor).astype(out[name].dtype)
    return out
```

```python
import math
from contextlib import ExitStack

import concourse.bass as bass
from concourse import mybir

FP32 = mybir.dt.float32
BF16 = mybir.dt.bfloat16
INT32 = mybir.dt.int32
ALU = mybir.AluOpType
ACT = mybir.ActivationFunctionType

P = 128
EPS = 1e-5
MASKED = -1000000000.0
SLOTS = 2


def graph_layers(nc, io, out):
    x, adj = io["x"], io["adj"]
    G, N, D = x.shape
    T = N // P
    W = T * D
    R = T * N

    x_rows = x.rearrange("g (p t) d -> p g (t d)", t=T)
    adj_rows = adj.rearrange("g (p t) n -> p g (t n)", t=T)
    out_rows = out.rearrange("g (p t) d -> p g (t d)", t=T)

    SKEW = dict(stats0=0, mask=1, project=1, scores=2, attend=3, swish1=4, mlp1=5, swish2=6, mlp2=7,
                residual=8, relate=9, aggregate=10)
    LAST_SKEW = max(SKEW.values())
    FLAG_STEP = G + SKEW["scores"] + 1
    FIRST_LOOPED = (LAST_SKEW + SLOTS + SLOTS - 1) // SLOTS * SLOTS

    ctx = ExitStack()
    with ctx:
        def sb(name, shape, dtype=FP32):
            return ctx.enter_context(nc.sbuf_tensor(name, shape, dtype))

        def sem(name):
            return ctx.enter_context(nc.semaphore(name))

        x_all = sb("x_all", [P, G * W])
        x2_all = sb("x2_all", [P, G * W])
        adj_all = sb("adj_all", [P, G * R], INT32)

        Wq = sb("Wq", [P, D])
        Wk = sb("Wk", [P, D])
        Wv = sb("Wv", [P, D])
        W1 = sb("W1", [P, D])
        W2 = sb("W2", [P, D])
        Wl = sb("Wl", [P, D])
        Wg = sb("Wg", [P, D])
        ln_cols = sb("ln_cols", [P, 4])
        bias_rows = sb("bias_rows", [P, 4, D])
        lnf_w = sb("lnf_w", [P, D])
        lnf_b = sb("lnf_b", [P, D])

        QK = sb("QK", [P, D])
        WvT = sb("WvT", [P, D])
        W12T = sb("W12T", [P, 2, D])
        W12 = sb("W12", [P, 2, D])
        WgT = sb("WgT", [P, D])
        relW = sb("relW", [P, 2, D])
        ln_b_wide = sb("ln_b_wide", [P, 2, P])
        bias = sb("bias", [P, 4, D])
        bias_hi = sb("bias_hi", [P, 4, D], BF16)
        bias_mid = sb("bias_mid", [P, 4, D], BF16)
        bias_lo = sb("bias_lo", [P, 4, D], BF16)
        bias_rest = sb("bias_rest", [P, 4, D])
        bias1 = sb("bias1", [P, T, D], BF16)
        bias2 = sb("bias2", [P, T, D], BF16)
        biasR = sb("biasR", [P, T, 2, D], BF16)
        thirtysecond = sb("thirtysecond", [P, P], BF16)
        identity = sb("identity", [P, P])
        minus_half = sb("minus_half", [P, T])
        eps_1 = sb("eps_1", [P, T])
        eps_4 = sb("eps_4", [P, T])

        def slots(name, shape, dtype=FP32):
            return [sb(f"{name}{s}", [P, *shape], dtype) for s in range(SLOTS)]

        xn0 = slots("xn0", [T, D])
        hT = slots("hT", [N])
        qkv = slots("qkv", [2 * N])
        mask = slots("mask", [T, N])
        neg_max = slots("neg_max", [T])
        prob = slots("prob", [T, N])
        prob_sum = slots("prob_sum", [T])
        inv_sum = slots("inv_sum", [T])
        probT = slots("probT", [T, N])
        attn = slots("attn", [T, D])
        th1 = slots("th1", [T, D])
        s1 = slots("s1", [T, D])
        xn1 = slots("xn1", [T, D])
        n1T = slots("n1T", [N])
        th2 = slots("th2", [T, D])
        s2 = slots("s2", [T, D])
        xn2 = slots("xn2", [T, D])
        n2T = slots("n2T", [N])
        lnf = slots("lnf", [T, D])
        xn3 = slots("xn3", [T, D])
        h2T = slots("h2T", [N])
        th3 = slots("th3", [T, D])
        vals = slots("vals", [T, D])
        onehot = slots("onehot", [T, N])
        result = slots("result", [T, D])
        squares = bias_rest[:, :, :].rearrange("p a d -> p (a d)")
        square_sums = sb("square_sums", [P, G])
        square_max = sb("square_max", [P, 1])
        others_row = sb("others_row", [P, 2], BF16)
        others_flag = sb("others_flag", [1, 2], INT32)
        LN = ("0", "1", "2", "f", "3")
        stats = {n: slots(f"stats{n}", [T, 6]) for n in LN}
        mean_var = {n: slots(f"mean_var{n}", [T, 2]) for n in LN}
        var_eps = {n: slots(f"var_eps{n}", [T]) for n in LN}
        rstd = {n: slots(f"rstd{n}", [T]) for n in LN}

        def bank(name):
            return ctx.enter_context(nc.psum_tensor(name, [P, 512], FP32))

        ps_qkv = bank("ps_qkv")
        ps_scores = bank("ps_scores")
        ps_attn = bank("ps_attn")
        ps_mlp1 = bank("ps_mlp1")
        ps_mlp2 = bank("ps_mlp2")
        ps_rel = bank("ps_rel")
        ps_t13 = bank("ps_t13")
        ps_t2out = bank("ps_t2out")

        sums = x_all
        table = xn2[0]
        row_number, row_pick = n1T[0][:, 0:P], n2T[0][:, 0:P]
        counters = sb("counters", [P, 2])

        graph_in = [sem(f"graph_in{s}") for s in range(SLOTS)]
        result_out = [sem(f"result_out{s}") for s in range(SLOTS)]
        weights_in = sem("weights_in")
        consts_zeroed = sem("consts_zeroed")
        consts_done = sem("consts_done")
        prep_products = sem("prep_products")
        prep_copied = sem("prep_copied")
        prep_scaled = sem("prep_scaled")
        prep_products2 = sem("prep_products2")
        rel_gate_ready = sem("rel_gate_ready")
        bias_step = sem("bias_step")
        bias_ready = sem("bias_ready")

        stats_done = {n: sem(f"stats{n}_done") for n in LN}
        mean_var_done = {n: sem(f"mean_var{n}_done") for n in LN}
        eps_added = {n: sem(f"eps_added{n}") for n in LN}
        rstd_done = {n: sem(f"rstd{n}_done") for n in LN}
        norm_done = {n: sem(f"norm{n}_done") for n in LN}
        transposed = {n: sem(f"transposed{n}") for n in ("0", "1", "2", "3")}
        hT_ready = sem("hT_ready")
        qkv_done = sem("qkv_done")
        qkv_ready = sem("qkv_ready")
        mask_ready = sem("mask_ready")
        scores_done = sem("scores_done")
        softmax_in = sem("softmax_in")
        prob_ready = sem("prob_ready")
        probT_done = sem("probT_done")
        probT_ready = sem("probT_ready")
        attn_done = sem("attn_done")
        inv_sum_ready = sem("inv_sum_ready")
        attn_ready = sem("attn_ready")
        tanh1_done = sem("tanh1_done")
        swish1_done = sem("swish1_done")
        n1T_ready = sem("n1T_ready")
        mlp1_done = sem("mlp1_done")
        tanh2_done = sem("tanh2_done")
        swish2_done = sem("swish2_done")
        n2T_ready = sem("n2T_ready")
        mlp2_done = sem("mlp2_done")
        lnfw_done = sem("lnfw_done")
        x_plus_b_ready = sem("x_plus_b_ready")
        x2_ready = sem("x2_ready")
        h2T_ready = sem("h2T_ready")
        rel_done = sem("rel_done")
        tanh3_done = sem("tanh3_done")
        vals_ready = sem("vals_ready")
        onehot_ready = sem("onehot_ready")
        aggregated = sem("aggregated")
        result_ready = sem("result_ready")
        squares_summed = sem("squares_summed")
        square_max_ready = sem("square_max_ready")
        others_row_ready = sem("others_row_ready")
        others_counted = sem("others_counted")
        flag_ready = sem("flag_ready")
        pass_weights_in = sem("pass_weights_in")
        pass_transposed = sem("pass_transposed")
        pass_copied = sem("pass_copied")
        pass_gated = sem("pass_gated")
        pass_ready = sem("pass_ready")
        table_cleared = sem("table_cleared")
        rows_numbered = sem("rows_numbered")
        node_copied = sem("node_copied")
        node_stats = sem("node_stats")
        node_mean_var = sem("node_mean_var")
        node_eps_added = sem("node_eps_added")
        node_rstd = sem("node_rstd")
        node_normalized = sem("node_normalized")
        node_transposed = sem("node_transposed")
        node_ready = sem("node_ready")
        counters_set = sem("counters_set")
        row_picked = sem("row_picked")
        edges_ready = sem("edges_ready")
        edges_transposed = sem("edges_transposed")
        edges_copied = sem("edges_copied")
        gates_done = sem("gates_done")
        gates_tanh = sem("gates_tanh")
        messages_ready = sem("messages_ready")
        messages_summed = sem("messages_summed")
        sum_added = sem("sum_added")
        sum_halved = sem("sum_halved")
        general_ready = sem("general_ready")
        general_out = sem("general_out")
        waits_taken = sem("waits_taken")

        def run(engine, step):
            for i in range(FIRST_LOOPED):
                step(i, i % SLOTS)
            with engine.Fori(FIRST_LOOPED, G - SLOTS + 1, SLOTS) as i:
                for u in range(SLOTS):
                    step(i + u, u)
            for i in range(G, G + LAST_SKEW):
                step(i, i % SLOTS)

        def has(i, stage):
            return not isinstance(i, int) or 0 <= i - SKEW[stage] < G

        def wait(engine, semaphore, count):
            if not isinstance(count, int):
                engine.wait_ge(semaphore, count)
            elif count > 0:
                engine.wait_ge(semaphore, min(count, G))

        def slot(stage, u):
            return (u - SKEW[stage]) % SLOTS

        def graph(tensor, g, width):
            return tensor[:, bass.ds(g * width, width)]

        def tiles(ap):
            return ap.rearrange("p (t d) -> p t d", t=T)

        RELATIONS = io["L1_gnn_b_fwd"].shape[0]
        PASSES = (("fwd", 2, RELATIONS, True), ("bwd", 2, RELATIONS, False), ("loop", 1, 1, False))

        def taken(engine, semaphore, count):
            engine.wait_ge(semaphore, count)
            engine.sem_inc(waits_taken, 1)

        def if_others(engine, body):
            engine.wait_ge(flag_ready, 1)
            others = engine.value_load(others_flag[0:1, 0:1], min_val=0, max_val=P)
            with engine.If(others > 0):
                engine.wait_ge(result_ready, G)
                body()

        def over_passes(engine, per_pass, per_graph, per_relation, after_graph=None):
            graphs = relations = 0
            for d, (name, first, number, rows_receive) in enumerate(PASSES):
                if per_pass:
                    per_pass(d, name, first)
                if per_graph or per_relation:
                    with engine.Fori(0, G) as g:
                        k = g + graphs
                        if per_graph:
                            per_graph(g, k, first)
                        if per_relation:
                            with engine.Fori(0, number) as r:
                                per_relation(g, g * number + r + relations, rows_receive)
                        if after_graph:
                            after_graph(d, g)
                graphs += G
                relations += G * number

        block = ctx.enter_context(nc.Block())

        @block.sync
        def _(sp):
            def load(g, s):
                wait(sp, stats_done["0"], g - 1)
                sp.dma_start(graph(x_all, g, W), x_rows[:, bass.ds(g, 1), :].rearrange("p g w -> p (g w)")).then_inc(graph_in[s], 16)
                sp.dma_start(graph(adj_all, g, R), adj_rows[:, bass.ds(g, 1), :].rearrange("p g w -> p (g w)")).then_inc(graph_in[s], 16)

            def store(g, s):
                wait(sp, result_ready, g + 1)
                sp.dma_start(out_rows[:, bass.ds(g, 1), :].rearrange("p g w -> p (g w)"), result[s][:, :, :].rearrange("p t d -> p (t d)")).then_inc(result_out[s], 16)

            for g in range(SLOTS):
                load(g, g)

            def step(i, u):
                if not isinstance(i, int) or i + SLOTS < G:
                    load(i + SLOTS, u)
                if has(i, "aggregate"):
                    store(i - SKEW["aggregate"], slot("aggregate", u))

            for i in range(FIRST_LOOPED):
                step(i, i % SLOTS)
            with sp.Fori(FIRST_LOOPED, G - 2 * SLOTS + 1, SLOTS) as i:
                for u in range(SLOTS):
                    step(i + u, u)
            for i in range(G - SLOTS, G + LAST_SKEW):
                step(i, i % SLOTS)
            for s in range(SLOTS):
                sp.wait_ge(result_out[s], 16 * (G // SLOTS))

            def general():
                def load_weights(d, name, first):
                    sp.wait_ge(table_cleared, d + 1)
                    number = io[f"L1_gnn_b_{name}"].shape[0]
                    sp.dma_start(Wl[:, :], io[f"L1_gnn_W_{name}"]).then_inc(pass_weights_in, 16)
                    sp.dma_start(Wg[:, :], io[f"L1_gnn_Wg_{name}"]).then_inc(pass_weights_in, 16)
                    sp.dma_start(table[0:number, 0, :], io[f"L1_gnn_b_{name}"]).then_inc(pass_weights_in, 16)
                    sp.dma_start(table[0:number, 1, :], io[f"L1_gnn_bg_{name}"]).then_inc(pass_weights_in, 16)

                over_passes(sp, load_weights, None, None)
                with sp.Fori(0, G) as g:
                    sp.wait_ge(general_ready, g + 1)
                    sp.dma_start(out_rows[:, bass.ds(g, 1), :].rearrange("p g w -> p (g w)"),
                                 result[0][:, :, :].rearrange("p t d -> p (t d)")).then_inc(general_out, 16)
                sp.wait_ge(general_out, 16 * G)

            if_others(sp, general)

        @block.gpsimd
        def _(pool):
            nc.gpsimd.memset(identity[:, :], 0.0).then_inc(consts_zeroed, 1)
            nc.gpsimd.memset(thirtysecond[:, :], 1 / 32).then_inc(consts_done, 1)
            nc.gpsimd.memset(minus_half[:, :], -0.5).then_inc(consts_done, 1)
            nc.gpsimd.memset(eps_1[:, :], EPS).then_inc(consts_done, 1)
            nc.gpsimd.memset(eps_4[:, :], 4 * EPS).then_inc(consts_done, 1)
            pool.wait_ge(consts_zeroed, 1)
            nc.gpsimd.affine_select(out=identity[:, :], in_=identity[:, :], compare_op=ALU.not_equal, fill=1.0,
                                    base=0, pattern=[[-1, P]], channel_multiplier=1).then_inc(consts_done, 1)
            pool.wait_ge(consts_done, 5)
            pool.wait_ge(weights_in, 16 * WEIGHT_LOADS)

            def inverse_std(n, g, s, eps):
                wait(pool, mean_var_done[n], g + 1)
                nc.gpsimd.tensor_tensor(var_eps[n][s][:, :], mean_var[n][s][:, :, 1], eps[:, :], ALU.add).then_inc(eps_added[n], 1)
                wait(pool, eps_added[n], g + 1)
                nc.gpsimd.tensor_tensor(rstd[n][s][:, :], var_eps[n][s][:, :], minus_half[:, :], ALU.pow).then_inc(rstd_done[n], 1)

            def step(i, u):
                if has(i, "swish1"):
                    inverse_std("1", i - SKEW["swish1"], slot("swish1", u), eps_4)
                if has(i, "swish2"):
                    inverse_std("2", i - SKEW["swish2"], slot("swish2", u), eps_4)
                if has(i, "mlp2"):
                    g, s = i - SKEW["mlp2"], slot("mlp2", u)
                    nc.gpsimd.tensor_tensor(tiles(graph(x_all, g, W)), tiles(graph(x_all, g, W)),
                                            lnf_b[:, :].unsqueeze(1).to_broadcast([P, T, D]), ALU.add).then_inc(x_plus_b_ready, 1)
                    inverse_std("f", g, s, eps_1)
                if has(i, "stats0"):
                    inverse_std("0", i - SKEW["stats0"], slot("stats0", u), eps_1)
                if has(i, "residual"):
                    inverse_std("3", i - SKEW["residual"], slot("residual", u), eps_1)

            run(pool, step)

            def general():
                nc.gpsimd.iota(row_number, pattern=[[0, P]], base=0, channel_multiplier=1,
                               allow_small_or_imprecise_dtypes=True).then_inc(rows_numbered, 1)

                def inverse_std(g, k, first):
                    pool.wait_ge(node_mean_var, k + 1)
                    nc.gpsimd.tensor_tensor(var_eps["3"][0][:, :], mean_var["3"][0][:, :, 1], eps_1[:, :], ALU.add).then_inc(node_eps_added, 1)
                    pool.wait_ge(node_eps_added, k + 1)
                    nc.gpsimd.tensor_tensor(rstd["3"][0][:, :], var_eps["3"][0][:, :], minus_half[:, :], ALU.pow).then_inc(node_rstd, 1)

                over_passes(pool, None, inverse_std, None)

            if_others(pool, general)

        @block.scalar
        def _(act):
            square = ((Wq, "L0_gnn_Wq"), (Wk, "L0_gnn_Wk"), (Wv, "L0_gnn_Wv"), (W1, "L0_gnn_W1"), (W2, "L0_gnn_W2"),
                      (Wl, "L1_gnn_W_loop"), (Wg, "L1_gnn_Wg_loop"))
            for tensor, name in square:
                act.dma_start(tensor[:, :], io[name]).then_inc(weights_in, 16)
            for c, name in enumerate(("L0_gnn_ln1_w", "L0_gnn_ln1_b", "L0_gnn_ln2_w", "L0_gnn_ln2_b")):
                act.dma_start(ln_cols[:, c:c + 1], io[name].unsqueeze(1)).then_inc(weights_in, 16)
            rows = ((bias_rows[:, 0, :], io["L0_gnn_b1"]), (bias_rows[:, 1, :], io["L0_gnn_b2"]),
                    (bias_rows[:, 2, :], io["L1_gnn_b_loop"][0, :]), (bias_rows[:, 3, :], io["L1_gnn_bg_loop"][0, :]),
                    (lnf_w[:, :], io["L0_gnn_lnf_w"]), (lnf_b[:, :], io["L0_gnn_lnf_b"]))
            for to, row in rows:
                act.dma_start(to, row.partition_broadcast(P)).then_inc(weights_in, 16)

            act.wait_ge(prep_products, 1)
            nc.scalar.activation(QK[:, :], ps_qkv[:, 0:D], ACT.Copy, scale=1 / math.sqrt(D))
            nc.scalar.activation(WvT[:, :], ps_qkv[:, D:2 * D], ACT.Copy)
            nc.scalar.activation(W12T[:, :, :], ps_qkv[:, 2 * D:4 * D].rearrange("p (a d) -> p a d", a=2), ACT.Copy)
            nc.scalar.activation(relW[:, 0, :], ps_scores[:, 0:D], ACT.Copy, scale=0.5)
            nc.scalar.activation(WgT[:, :], ps_scores[:, D:2 * D], ACT.Copy).then_inc(prep_copied, 1)
            act.wait_ge(prep_products2, 1)
            nc.scalar.activation(relW[:, 1, :], ps_scores[:, 0:D], ACT.Copy).then_inc(rel_gate_ready, 1)

            def step(i, u):
                if has(i, "swish1"):
                    g, s = i - SKEW["swish1"], slot("swish1", u)
                    wait(act, attn_ready, g + 1)
                    nc.scalar.activation(th1[s][:, :, :], attn[s][:, :, :], ACT.Tanh, scale=0.5).then_inc(tanh1_done, 1)
                if has(i, "swish2"):
                    g, s = i - SKEW["swish2"], slot("swish2", u)
                    wait(act, mlp1_done, g + 1)
                    nc.scalar.activation(th2[s][:, :, :], tiles(ps_mlp1[:, 0:W]), ACT.Tanh, scale=0.5).then_inc(tanh2_done, 1)
                if has(i, "aggregate"):
                    g, s = i - SKEW["aggregate"], slot("aggregate", u)
                    wait(act, rel_done, g + 1)
                    nc.scalar.activation(th3[s][:, :, :], ps_rel[:, :].rearrange("p (t a d) -> p t a d", t=T, a=2)[:, :, 1, :],
                                         ACT.Tanh, scale=0.5).then_inc(tanh3_done, 1)
                if has(i, "mask"):
                    g, s = i - SKEW["mask"], slot("mask", u)
                    wait(act, mask_ready, g + 1)
                    nc.scalar.activation(squares, graph(adj_all, g, R), ACT.Square, bias=minus_half[:, 0:1],
                                         accum_out=square_sums[:, bass.ds(g, 1)]).then_inc(squares_summed, 1)
                if has(i, "attend"):
                    g, s = i - SKEW["attend"], slot("attend", u)
                    wait(act, probT_done, g + 1)
                    nc.scalar.activation(probT[s][:, :, :].rearrange("p t n -> p (t n)"), ps_attn[:, :], ACT.Copy).then_inc(probT_ready, 1)
                if has(i, "project"):
                    g, s = i - SKEW["project"], slot("project", u)
                    wait(act, transposed["0"], g + 1)
                    nc.scalar.activation(hT[s][:, :], ps_qkv[:, 0:N], ACT.Relu).then_inc(hT_ready, 1)
                if has(i, "mlp1"):
                    g, s = i - SKEW["mlp1"], slot("mlp1", u)
                    wait(act, transposed["1"], g + 1)
                    nc.scalar.activation(n1T[s][:, :], ps_t13[:, 0:N], ACT.Copy).then_inc(n1T_ready, 1)
                if has(i, "relate"):
                    g, s = i - SKEW["relate"], slot("relate", u)
                    wait(act, transposed["3"], g + 1)
                    nc.scalar.activation(h2T[s][:, :], ps_t13[:, 0:N], ACT.Relu).then_inc(h2T_ready, 1)
                if has(i, "mlp2"):
                    g, s = i - SKEW["mlp2"], slot("mlp2", u)
                    wait(act, transposed["2"], g + 1)
                    nc.scalar.activation(n2T[s][:, :], ps_t2out[:, 0:N], ACT.Copy).then_inc(n2T_ready, 1)
                if has(i, "project"):
                    g, s = i - SKEW["project"], slot("project", u)
                    wait(act, qkv_done, g + 1)
                    nc.scalar.activation(qkv[s][:, :], ps_qkv[:, :], ACT.Copy).then_inc(qkv_ready, 1)
                if has(i, "scores"):
                    g, s = i - SKEW["scores"], slot("scores", u)
                    wait(act, softmax_in, g + 1)
                    nc.scalar.activation(prob[s][:, 0, :], mask[s][:, 0, :], ACT.Exp, bias=neg_max[s][:, 0:1], scale=-1.0,
                                         accum_out=prob_sum[s][:, 0:1])
                    nc.scalar.activation(prob[s][:, 1, :], mask[s][:, 1, :], ACT.Exp, bias=neg_max[s][:, 1:2], scale=-1.0,
                                         accum_out=prob_sum[s][:, 1:2]).then_inc(prob_ready, 1)

            run(act, step)

            def general():
                def copy_weights(d, name, first):
                    act.wait_ge(pass_transposed, d + 1)
                    nc.scalar.activation(relW[:, 0, :], ps_scores[:, 0:D], ACT.Copy)
                    nc.scalar.activation(WgT[:, :], ps_scores[:, D:2 * D], ACT.Copy).then_inc(pass_copied, 1)
                    act.wait_ge(pass_gated, d + 1)
                    nc.scalar.activation(relW[:, 1, :], ps_scores[:, 0:D], ACT.Copy).then_inc(pass_ready, 1)

                def copy_nodes(g, k, first):
                    act.wait_ge(node_transposed, k + 1)
                    nc.scalar.activation(h2T[0][:, :], ps_t13[:, 0:N], ACT.Relu).then_inc(node_ready, 1)

                def relation(g, n, rows_receive):
                    if rows_receive:
                        act.wait_ge(edges_transposed, n + 1)
                        nc.scalar.activation(probT[0][:, :, :].rearrange("p t n -> p (t n)"), ps_attn[:, :], ACT.Copy).then_inc(edges_copied, 1)
                    act.wait_ge(gates_done, n + 1)
                    nc.scalar.activation(th3[0][:, :, :], ps_rel[:, :].rearrange("p (t a d) -> p t a d", t=T, a=2)[:, :, 1, :],
                                         ACT.Tanh, scale=0.5).then_inc(gates_tanh, 1)

                over_passes(act, copy_weights, copy_nodes, relation)

            if_others(act, general)

        @block.vector
        def _(dve):
            v = nc.vector
            dve.wait_ge(weights_in, 16 * WEIGHT_LOADS)
            for a in range(2):
                last = v.tensor_copy(ln_b_wide[:, a, :], ln_cols[:, 2 * a + 1:2 * a + 2].to_broadcast([P, P]))
            last.then_inc(prep_scaled, 1)
            dve.wait_ge(prep_copied, 1)
            for a in range(2):
                last = v.tensor_scalar(W12[:, a, :], W12T[:, a, :], ln_cols[:, 2 * a:2 * a + 1], None, ALU.mult)
            last.then_inc(prep_scaled, 1)
            v.tensor_scalar(bias[:, 2, :], bias_rows[:, 2, :], 0.5, None, ALU.mult)
            v.tensor_copy(bias[:, 3, :], bias_rows[:, 3, :])
            dve.wait_ge(prep_products2, 1)
            v.tensor_tensor(bias[:, 0:2, :], ps_qkv[:, 0:2 * D].rearrange("p (a d) -> p a d", a=2), bias_rows[:, 0:2, :],
                            ALU.add).then_inc(bias_step, 1)
            dve.wait_ge(bias_step, 1)
            v.tensor_copy(bias_hi[:, :, :], bias[:, :, :]).then_inc(bias_step, 1)
            dve.wait_ge(bias_step, 2)
            v.tensor_tensor(bias_rest[:, :, :], bias[:, :, :], bias_hi[:, :, :], ALU.subtract).then_inc(bias_step, 1)
            dve.wait_ge(bias_step, 3)
            v.tensor_copy(bias_mid[:, :, :], bias_rest[:, :, :]).then_inc(bias_step, 1)
            dve.wait_ge(bias_step, 4)
            v.tensor_tensor(bias_lo[:, :, :], bias_rest[:, :, :], bias_mid[:, :, :], ALU.subtract).then_inc(bias_step, 1)
            dve.wait_ge(bias_step, 5)
            for q, part in enumerate((bias_hi, bias_mid, bias_lo, None)):
                rows = slice(32 * q, 32 * q + 32)
                for t in range(T):
                    for to, frm in ((bias1[rows, t, :], 0), (bias2[rows, t, :], 1), (biasR[rows, t, 0, :], 2), (biasR[rows, t, 1, :], 3)):
                        if part is None:
                            last = v.memset(to, 0.0)
                        else:
                            last = v.tensor_copy(to, part[rows, frm, :])
            last.then_inc(bias_ready, 1)

            def statistics(n, source, g, s):
                for t in range(T):
                    last = v.bn_stats(stats[n][s][:, t, :], source(t))
                last.then_inc(stats_done[n], 1)

            def mean_variance(n, g, s):
                wait(dve, stats_done[n], g + 1)
                dve.sem_inc(waits_taken, 1)
                for t in range(T):
                    last = v.bn_aggr(mean_var[n][s][:, t, :], stats[n][s][:, t, :])
                last.then_inc(mean_var_done[n], 1)

            def normalize(n, to, source, g, s):
                wait(dve, rstd_done[n], g + 1)
                for t in range(T):
                    last = v.tensor_scalar(to[s][:, t, :], source(t), mean_var[n][s][:, t, 0:1], rstd[n][s][:, t:t + 1],
                                           ALU.subtract, ALU.mult)
                last.then_inc(norm_done[n], 1)

            def flag_others():
                dve.wait_ge(squares_summed, G)
                v.reduce_max(square_max[:, :], square_sums[:, :], axis=mybir.AxisListType.X).then_inc(square_max_ready, 1)
                dve.wait_ge(square_max_ready, 1)
                for c in range(2):
                    last = v.tensor_scalar(others_row[:, c:c + 1], square_max[:, :], R / 4 + 1, None, ALU.is_gt)
                last.then_inc(others_row_ready, 1)
                dve.wait_ge(others_counted, 1)
                v.tensor_scalar(others_flag[:, :], ps_scores[0:1, 0:2], 32.0, None, ALU.mult).then_inc(flag_ready, 1)

            def step(i, u):
                if isinstance(i, int) and i == FLAG_STEP:
                    flag_others()
                if has(i, "project"):
                    g, s = i - SKEW["project"], slot("project", u)
                    normalize("0", xn0, lambda t: graph(x_all, g * T + t, D), g, s)
                if has(i, "mlp1"):
                    g, s = i - SKEW["mlp1"], slot("mlp1", u)
                    normalize("1", xn1, lambda t: s1[s][:, t, :], g, s)
                if has(i, "relate"):
                    g, s = i - SKEW["relate"], slot("relate", u)
                    normalize("3", xn3, lambda t: graph(x2_all, g * T + t, D), g, s)
                if has(i, "mlp2"):
                    g, s = i - SKEW["mlp2"], slot("mlp2", u)
                    normalize("2", xn2, lambda t: s2[s][:, t, :], g, s)
                if has(i, "residual"):
                    g, s = i - SKEW["residual"], slot("residual", u)
                    normalize("f", lnf, lambda t: ps_mlp2[:, t * D:(t + 1) * D], g, s)
                if has(i, "mask"):
                    g, s = i - SKEW["mask"], slot("mask", u)
                    dve.wait_ge(graph_in[s], graphs_in(g, s))
                    wait(dve, prob_ready, g - 1)
                    v.tensor_scalar(mask[s][:, :, :].rearrange("p t (s q) -> p t s q", s=T),
                                    graph(adj_all, g, R).rearrange("p (t q s) -> p t s q", t=T, s=T),
                                    0, MASKED, ALU.is_equal, ALU.mult).then_inc(mask_ready, 1)
                if has(i, "relate"):
                    g, s = i - SKEW["relate"], slot("relate", u)
                    v.tensor_scalar(onehot[s][:, :, :].rearrange("p t (s q) -> p t s q", s=T),
                                    graph(adj_all, g, R).rearrange("p (t q s) -> p t s q", t=T, s=T),
                                    1, None, ALU.is_equal).then_inc(onehot_ready, 1)
                if has(i, "swish1"):
                    g, s = i - SKEW["swish1"], slot("swish1", u)
                    wait(dve, tanh1_done, g + 1)
                    v.scalar_tensor_tensor(s1[s][:, :, :], th1[s][:, :, :], 1.0, attn[s][:, :, :], ALU.add, ALU.mult).then_inc(swish1_done, 1)
                if has(i, "swish2"):
                    g, s = i - SKEW["swish2"], slot("swish2", u)
                    wait(dve, tanh2_done, g + 1)
                    v.scalar_tensor_tensor(s2[s][:, :, :], th2[s][:, :, :], 1.0, tiles(ps_mlp1[:, 0:W]), ALU.add, ALU.mult).then_inc(swish2_done, 1)
                if has(i, "aggregate"):
                    g, s = i - SKEW["aggregate"], slot("aggregate", u)
                    wait(dve, tanh3_done, g + 1)
                    v.scalar_tensor_tensor(vals[s][:, :, :], th3[s][:, :, :], 1.0,
                                           ps_rel[:, :].rearrange("p (t a d) -> p t a d", t=T, a=2)[:, :, 0, :],
                                           ALU.add, ALU.mult).then_inc(vals_ready, 1)
                if has(i, "swish1"):
                    g, s = i - SKEW["swish1"], slot("swish1", u)
                    wait(dve, swish1_done, g + 1)
                    statistics("1", lambda t: s1[s][:, t, :], g, s)
                if has(i, "residual"):
                    g, s = i - SKEW["residual"], slot("residual", u)
                    wait(dve, norm_done["f"], g + 1)
                    v.tensor_tensor(lnf[s][:, :, :], lnf[s][:, :, :], lnf_w[:, :].unsqueeze(1).to_broadcast([P, T, D]),
                                    ALU.mult).then_inc(lnfw_done, 1)
                if has(i, "swish2"):
                    g, s = i - SKEW["swish2"], slot("swish2", u)
                    wait(dve, swish2_done, g + 1)
                    statistics("2", lambda t: s2[s][:, t, :], g, s)
                if has(i, "swish1"):
                    mean_variance("1", i - SKEW["swish1"], slot("swish1", u))
                if has(i, "residual"):
                    g, s = i - SKEW["residual"], slot("residual", u)
                    wait(dve, lnfw_done, g + 1)
                    wait(dve, x_plus_b_ready, g + 1)
                    v.tensor_tensor(tiles(graph(x2_all, g, W)), lnf[s][:, :, :], tiles(graph(x_all, g, W)), ALU.add).then_inc(x2_ready, 1)
                if has(i, "swish2"):
                    mean_variance("2", i - SKEW["swish2"], slot("swish2", u))
                if has(i, "stats0"):
                    g, s = i - SKEW["stats0"], slot("stats0", u)
                    dve.wait_ge(graph_in[s], graphs_in(g, s))
                    statistics("0", lambda t: graph(x_all, g * T + t, D), g, s)
                if has(i, "residual"):
                    g, s = i - SKEW["residual"], slot("residual", u)
                    wait(dve, x2_ready, g + 1)
                    statistics("3", lambda t: graph(x2_all, g * T + t, D), g, s)
                if has(i, "stats0"):
                    mean_variance("0", i - SKEW["stats0"], slot("stats0", u))
                if has(i, "scores"):
                    g, s = i - SKEW["scores"], slot("scores", u)
                    wait(dve, scores_done, g + 1)
                    wait(dve, mask_ready, g + 1)
                    dve.sem_inc(waits_taken, 1)
                    for t in range(T):
                        last = v.tensor_tensor_reduce(out=mask[s][:, t, :], in0=ps_scores[:, t * N:(t + 1) * N], in1=mask[s][:, t, :],
                                                      scale=-1.0, scalar=3.0e38, op0=ALU.add, op1=ALU.min,
                                                      accum_out=neg_max[s][:, t:t + 1])
                    last.then_inc(softmax_in, 1)
                if has(i, "residual"):
                    mean_variance("3", i - SKEW["residual"], slot("residual", u))
                if has(i, "attend"):
                    g, s = i - SKEW["attend"], slot("attend", u)
                    wait(dve, prob_ready, g + 1)
                    v.reciprocal(inv_sum[s][:, :], prob_sum[s][:, :]).then_inc(inv_sum_ready, 1)
                if has(i, "mlp2"):
                    g, s = i - SKEW["mlp2"], slot("mlp2", u)
                    wait(dve, mlp2_done, g + 1)
                    statistics("f", lambda t: ps_mlp2[:, t * D:(t + 1) * D], g, s)
                if has(i, "attend"):
                    g, s = i - SKEW["attend"], slot("attend", u)
                    wait(dve, inv_sum_ready, g + 1)
                    wait(dve, attn_done, g + 1)
                    v.tensor_tensor(attn[s][:, :, :], tiles(ps_attn[:, 0:W]), inv_sum[s][:, :].unsqueeze(2).to_broadcast([P, T, D]),
                                    ALU.mult).then_inc(attn_ready, 1)
                if has(i, "mlp2"):
                    mean_variance("f", i - SKEW["mlp2"], slot("mlp2", u))
                if has(i, "aggregate"):
                    g, s = i - SKEW["aggregate"], slot("aggregate", u)
                    wait(dve, aggregated, g + 1)
                    if not isinstance(g, int) or g >= SLOTS:
                        dve.wait_ge(result_out[s], results_out(g, s))
                    v.scalar_tensor_tensor(result[s][:, :, :], tiles(ps_t2out[:, 0:W]), 0.0, tiles(graph(x2_all, g, W)),
                                           ALU.max, ALU.add).then_inc(result_ready, 1)

            run(dve, step)

            def general():
                for s in range(SLOTS):
                    dve.wait_ge(result_out[s], 16 * (G // SLOTS))
                dve.wait_ge(rows_numbered, 1)
                v.memset(sums[:, :], 0.0)

                def clear_table(d, name, first):
                    v.memset(table[:, :, :], 0.0).then_inc(table_cleared, 1)

                def normalize_nodes(g, k, first):
                    v.tensor_scalar(s2[0][:, :, :], tiles(graph(x2_all, g, W)), 1.0, None, ALU.mult).then_inc(node_copied, 1)
                    dve.wait_ge(node_copied, k + 1)
                    for t in range(T):
                        last = v.bn_stats(stats["3"][0][:, t, :], s2[0][:, t, :])
                    last.then_inc(node_stats, 1)
                    taken(dve, node_stats, k + 1)
                    for t in range(T):
                        last = v.bn_aggr(mean_var["3"][0][:, t, :], stats["3"][0][:, t, :])
                    last.then_inc(node_mean_var, 1)
                    dve.wait_ge(node_rstd, k + 1)
                    for t in range(T):
                        last = v.tensor_scalar(xn3[0][:, t, :], s2[0][:, t, :], mean_var["3"][0][:, t, 0:1], rstd["3"][0][:, t:t + 1],
                                               ALU.subtract, ALU.mult)
                    last.then_inc(node_normalized, 1)
                    v.memset(counters[:, 0:1], 0.0)
                    v.memset(counters[:, 1:2], float(first)).then_inc(counters_set, 1)
                    taken(dve, counters_set, k + 1)

                def relation(g, n, rows_receive):
                    v.tensor_scalar(row_pick, row_number, counters[:, 0:1], None, ALU.is_equal).then_inc(row_picked, 1)
                    v.tensor_scalar(onehot[0][:, :, :].rearrange("p t (s q) -> p t s q", s=T),
                                    graph(adj_all, g, R).rearrange("p (t q s) -> p t s q", t=T, s=T),
                                    counters[:, 1:2], None, ALU.is_equal).then_inc(edges_ready, 1)
                    dve.wait_ge(gates_tanh, n + 1)
                    v.scalar_tensor_tensor(vals[0][:, :, :], th3[0][:, :, :], 1.0,
                                           ps_rel[:, :].rearrange("p (t a d) -> p t a d", t=T, a=2)[:, :, 0, :],
                                           ALU.add, ALU.mult).then_inc(messages_ready, 1)
                    dve.wait_ge(edges_ready, n + 1)
                    v.tensor_scalar(counters[:, :], counters[:, :], 1.0, None, ALU.add)
                    dve.wait_ge(messages_summed, n + 1)
                    v.tensor_tensor(tiles(graph(sums, g, W)), tiles(ps_t2out[:, 0:W]), tiles(graph(sums, g, W)), ALU.add).then_inc(sum_added, 1)
                    taken(dve, sum_added, n + 1)

                def finish(d, g):
                    if d < len(PASSES) - 1:
                        return
                    v.tensor_scalar(s2[0][:, :, :], tiles(graph(sums, g, W)), 0.5, 0.0, ALU.mult, ALU.max).then_inc(sum_halved, 1)
                    dve.wait_ge(sum_halved, g + 1)
                    v.tensor_tensor(result[0][:, :, :], s2[0][:, :, :], tiles(graph(x2_all, g, W)), ALU.add).then_inc(general_ready, 1)
                    dve.wait_ge(general_out, (g + 1) * 16)

                over_passes(dve, clear_table, normalize_nodes, relation, finish)

            if_others(dve, general)

        @block.tensor
        def _(pe):
            mm, transpose = nc.tensor.matmul, nc.tensor.transpose
            pe.wait_ge(consts_done, 5)
            pe.wait_ge(weights_in, 16 * WEIGHT_LOADS)
            mm(ps_qkv[:, 0:D], Wq[:, :], Wk[:, :], start=True, stop=True)
            transpose(ps_qkv[:, D:2 * D], Wv[:, :], identity[:, :])
            transpose(ps_qkv[:, 2 * D:3 * D], W1[:, :], identity[:, :])
            transpose(ps_qkv[:, 3 * D:4 * D], W2[:, :], identity[:, :])
            transpose(ps_scores[:, 0:D], Wl[:, :], identity[:, :])
            transpose(ps_scores[:, D:2 * D], Wg[:, :], identity[:, :]).then_inc(prep_products, 1)
            pe.wait_ge(prep_copied, 1)
            pe.wait_ge(prep_scaled, 1)
            for a in range(2):
                mm(ps_qkv[:, a * D:(a + 1) * D], ln_b_wide[:, a, :], W12T[:, a, :], start=True, stop=True)
            mm(ps_scores[:, 0:D], Wl[:, :], WgT[:, :], start=True, stop=True).then_inc(prep_products2, 1)
            pe.wait_ge(prep_scaled, 2)
            pe.wait_ge(rel_gate_ready, 1)
            pe.wait_ge(bias_ready, 1)

            def transpose_rows(bank, source, n):
                for t in range(T):
                    last = transpose(bank[:, t * P:(t + 1) * P], source[:, t, :], identity[:, :])
                last.then_inc(transposed[n], 1)

            def linear(bank, xT, weights, bias_parts, done):
                width = weights.shape[1]
                mm(bank[:, 0:T * width], thirtysecond[:, :], bias_parts, start=True, stop=False, skip_group_check=True)
                for t in range(T):
                    last = mm(bank[:, t * width:(t + 1) * width], xT[:, t * P:(t + 1) * P], weights, start=False, stop=True,
                              skip_group_check=True)
                last.then_inc(done, 1)

            def step(i, u):
                if isinstance(i, int) and i == FLAG_STEP:
                    pe.wait_ge(others_row_ready, 1)
                    mm(ps_scores[:, 0:2], thirtysecond[:, :], others_row[:, :], start=True, stop=True).then_inc(others_counted, 1)
                if has(i, "attend"):
                    g, s = i - SKEW["attend"], slot("attend", u)
                    wait(pe, prob_ready, g + 1)
                    wait(pe, attn_ready, g)
                    for c in range(T):
                        for t in range(T):
                            last = transpose(ps_attn[:, c * N + t * P:c * N + (t + 1) * P], prob[s][:, t, c * P:(c + 1) * P], identity[:, :])
                    last.then_inc(probT_done, 1)
                if has(i, "scores"):
                    g, s = i - SKEW["scores"], slot("scores", u)
                    wait(pe, qkv_ready, g + 1)
                    wait(pe, softmax_in, g)
                    for t in range(T):
                        last = mm(ps_scores[:, t * N:(t + 1) * N], qkv[s][:, t * P:(t + 1) * P], hT[s][:, :], start=True, stop=True)
                    last.then_inc(scores_done, 1)
                if has(i, "project"):
                    g, s = i - SKEW["project"], slot("project", u)
                    wait(pe, norm_done["0"], g + 1)
                    transpose_rows(ps_qkv, xn0[s], "0")
                if has(i, "mlp1"):
                    g, s = i - SKEW["mlp1"], slot("mlp1", u)
                    wait(pe, norm_done["1"], g + 1)
                    wait(pe, h2T_ready, i - SKEW["relate"])
                    transpose_rows(ps_t13, xn1[s], "1")
                if has(i, "mlp2"):
                    g, s = i - SKEW["mlp2"], slot("mlp2", u)
                    wait(pe, norm_done["2"], g + 1)
                    wait(pe, result_ready, i - SKEW["aggregate"])
                    transpose_rows(ps_t2out, xn2[s], "2")
                if has(i, "attend"):
                    g, s = i - SKEW["attend"], slot("attend", u)
                    wait(pe, probT_ready, g + 1)
                    for t in range(T):
                        for c in range(T):
                            last = mm(ps_attn[:, t * D:(t + 1) * D], probT[s][:, c, t * P:(t + 1) * P],
                                      qkv[s][:, N + c * D:N + (c + 1) * D], start=(c == 0), stop=(c == T - 1))
                    last.then_inc(attn_done, 1)
                if has(i, "relate"):
                    g, s = i - SKEW["relate"], slot("relate", u)
                    wait(pe, norm_done["3"], g + 1)
                    wait(pe, n1T_ready, i - SKEW["mlp1"] + 1)
                    transpose_rows(ps_t13, xn3[s], "3")
                if has(i, "project"):
                    g, s = i - SKEW["project"], slot("project", u)
                    wait(pe, hT_ready, g + 1)
                    mm(ps_qkv[:, 0:N], QK[:, :], hT[s][:, :], start=True, stop=True)
                    for t in range(T):
                        last = mm(ps_qkv[:, N + t * D:N + (t + 1) * D], hT[s][:, t * P:(t + 1) * P], WvT[:, :], start=True, stop=True)
                    last.then_inc(qkv_done, 1)
                if has(i, "mlp1"):
                    g, s = i - SKEW["mlp1"], slot("mlp1", u)
                    wait(pe, n1T_ready, g + 1)
                    wait(pe, swish2_done, g)
                    linear(ps_mlp1, n1T[s], W12[:, 0, :], bias1[:, :, :].rearrange("p t d -> p (t d)"), mlp1_done)
                if has(i, "mlp2"):
                    g, s = i - SKEW["mlp2"], slot("mlp2", u)
                    wait(pe, n2T_ready, g + 1)
                    wait(pe, norm_done["f"], g)
                    linear(ps_mlp2, n2T[s], W12[:, 1, :], bias2[:, :, :].rearrange("p t d -> p (t d)"), mlp2_done)
                if has(i, "relate"):
                    g, s = i - SKEW["relate"], slot("relate", u)
                    wait(pe, h2T_ready, g + 1)
                    wait(pe, vals_ready, g)
                    linear(ps_rel, h2T[s], relW[:, :, :].rearrange("p a d -> p (a d)"),
                           biasR[:, :, :, :].rearrange("p t a d -> p (t a d)"), rel_done)
                if has(i, "aggregate"):
                    g, s = i - SKEW["aggregate"], slot("aggregate", u)
                    wait(pe, vals_ready, g + 1)
                    wait(pe, onehot_ready, g + 1)
                    wait(pe, n2T_ready, i - SKEW["mlp2"] + 1)
                    wait(pe, result_ready, g)
                    for t in range(T):
                        for c in range(T):
                            last = mm(ps_t2out[:, t * D:(t + 1) * D], onehot[s][:, c, t * P:(t + 1) * P], vals[s][:, c, :],
                                      start=(c == 0), stop=(c == T - 1))
                    last.then_inc(aggregated, 1)

            run(pe, step)

            def general():
                def prepare(d, name, first):
                    pe.wait_ge(pass_weights_in, 16 * 4 * (d + 1))
                    transpose(ps_scores[:, 0:D], Wl[:, :], identity[:, :])
                    transpose(ps_scores[:, D:2 * D], Wg[:, :], identity[:, :]).then_inc(pass_transposed, 1)
                    pe.wait_ge(pass_copied, d + 1)
                    mm(ps_scores[:, 0:D], Wl[:, :], WgT[:, :], start=True, stop=True).then_inc(pass_gated, 1)
                    pe.wait_ge(pass_ready, d + 1)

                def transpose_nodes(g, k, first):
                    pe.wait_ge(node_normalized, k + 1)
                    for t in range(T):
                        last = transpose(ps_t13[:, t * P:(t + 1) * P], xn3[0][:, t, :], identity[:, :])
                    last.then_inc(node_transposed, 1)
                    taken(pe, node_ready, k + 1)

                def relation(g, n, rows_receive):
                    pe.wait_ge(row_picked, n + 1)
                    weights, biases = (a[:, :, :].rearrange("p a d -> p (a d)") for a in (relW, table))
                    for t in range(T):
                        half = ps_rel[:, t * 2 * D:(t + 1) * 2 * D]
                        mm(half, row_pick, biases, start=True, stop=False)
                        last = mm(half, h2T[0][:, t * P:(t + 1) * P], weights, start=False, stop=True)
                    last.then_inc(gates_done, 1)
                    edges = onehot[0]
                    pe.wait_ge(edges_ready, n + 1)
                    if rows_receive:
                        for c in range(T):
                            for t in range(T):
                                last = transpose(ps_attn[:, c * N + t * P:c * N + (t + 1) * P], onehot[0][:, t, c * P:(c + 1) * P], identity[:, :])
                        last.then_inc(edges_transposed, 1)
                        pe.wait_ge(edges_copied, n + 1)
                        edges = probT[0]
                    pe.wait_ge(messages_ready, n + 1)
                    for t in range(T):
                        for c in range(T):
                            last = mm(ps_t2out[:, t * D:(t + 1) * D], edges[:, c, t * P:(t + 1) * P], vals[0][:, c, :],
                                      start=(c == 0), stop=(c == T - 1))
                    last.then_inc(messages_summed, 1)

                over_passes(pe, prepare, transpose_nodes, relation)

            if_others(pe, general)


WEIGHT_LOADS = 17


def graphs_in(g, s):
    return 16 * 2 * (g // SLOTS + 1) if isinstance(g, int) else (g - s) * (16 * 2 // SLOTS) + 16 * 2


def results_out(g, s):
    return 16 * (g // SLOTS) if isinstance(g, int) else (g - s) * (16 // SLOTS)


_INS = ["x", "adj", "L0_gnn_Wq", "L0_gnn_Wk", "L0_gnn_Wv", "L0_gnn_ln1_w", "L0_gnn_ln1_b", "L0_gnn_W1", "L0_gnn_b1",
        "L0_gnn_ln2_w", "L0_gnn_ln2_b", "L0_gnn_W2", "L0_gnn_b2", "L0_gnn_lnf_w", "L0_gnn_lnf_b",
        *(f"L1_gnn_{kind}_{name}" for kind in ("W", "Wg", "b", "bg") for name in ("fwd", "bwd", "loop"))]


def kernel(**inputs):
    import numpy as np
    import concourse.bacc as bacc
    from concourse.bass_utils import run_bass_kernel_spmd

    nc = bacc.Bacc("TRN2", target_bir_lowering=False, num_devices=1)
    arrays, io = {}, {}
    for name in _INS:
        a = np.ascontiguousarray(inputs[name])
        arrays[f"in_{name}"] = a
        io[name] = nc.dram_tensor(f"in_{name}", a.shape, mybir.dt.from_np(a.dtype), kind="ExternalInput").ap()
    out = nc.dram_tensor("out", arrays["in_x"].shape, FP32, kind="ExternalOutput").ap()
    graph_layers(nc, io, out)
    r = run_bass_kernel_spmd(nc, [arrays], core_ids=[0])
    return r.results[0]["out"]
```

```python
import math
from contextlib import ExitStack

import concourse.bass as bass
from concourse import mybir

FP32 = mybir.dt.float32
BF16 = mybir.dt.bfloat16
INT32 = mybir.dt.int32
ALU = mybir.AluOpType
ACT = mybir.ActivationFunctionType

P = 128
EPS = 1e-5
MASKED = -1000000000.0
SLOTS = 2


def graph_layers(nc, io, out):
    x, adj = io["x"], io["adj"]
    G, N, D = x.shape
    T = N // P
    W = T * D
    R = T * N

    x_rows = x.rearrange("g (p t) d -> p g (t d)", t=T)
    adj_rows = adj.rearrange("g (p t) n -> p g (t n)", t=T)
    out_rows = out.rearrange("g (p t) d -> p g (t d)", t=T)

    SKEW = dict(stats0=0, mean0=0, norm0=1, make_mask=1, copy_hT=2, copy_qkv=2, softmax_input=2, rstd0=2, transpose0=2, project=2, softmax=2, exponentials=3, inverse_sum=3, add_bias=3, scores=3, transpose_probs=3, copy_probT=4, scale_attn=4, swish1=4, stats1=4, mean1=4, attend=4, tanh1=5, norm1=6, copy_n1T=6, swish2=6, stats2=6, mean2=6, transpose1=6, mlp1=6, tanh2=7, rstd1=7, norm2=8, copy_n2T=8, statsf=8, meanf=8, normf=8, transpose2=8, mlp2=8, residual=9, stats3=9, mean3=9, norm3=9, rstd2=9, check=10, select_edges=10, rstdf=10, scale_f=10, transpose3=10, copy_h2T=11, tanh3=11, messages=11, add_messages=11, rstd3=11, relate=11, aggregate=11, result=11)
    LAST_SKEW = max(SKEW.values())
    FLAG_STEP = G + min(max(SKEW["softmax"], SKEW["check"]) + 1, LAST_SKEW)
    FIRST_LOOPED = (LAST_SKEW + SLOTS + SLOTS - 1) // SLOTS * SLOTS

    ctx = ExitStack()
    with ctx:
        def sb(name, shape, dtype=FP32):
            return ctx.enter_context(nc.sbuf_tensor(name, shape, dtype))

        def sem(name):
            return ctx.enter_context(nc.semaphore(name))

        x_all = sb("x_all", [P, G * W])
        x2_all = sb("x2_all", [P, G * W])
        adj_all = sb("adj_all", [P, G * R], INT32)

        Wq = sb("Wq", [P, D])
        Wk = sb("Wk", [P, D])
        Wv = sb("Wv", [P, D])
        W1 = sb("W1", [P, D])
        W2 = sb("W2", [P, D])
        Wl = sb("Wl", [P, D])
        Wg = sb("Wg", [P, D])
        ln_cols = sb("ln_cols", [P, 4])
        bias_rows = sb("bias_rows", [P, 4, D])
        lnf_w = sb("lnf_w", [P, D])
        lnf_b = sb("lnf_b", [P, D])

        QK = sb("QK", [P, D])
        WvT = sb("WvT", [P, D])
        W12T = sb("W12T", [P, 2, D])
        W12 = sb("W12", [P, 2, D])
        WgT = sb("WgT", [P, D])
        relW = sb("relW", [P, 2, D])
        ln_b_wide = sb("ln_b_wide", [P, 2, P])
        bias = sb("bias", [P, 4, D])
        bias_hi = sb("bias_hi", [P, 4, D], BF16)
        bias_mid = sb("bias_mid", [P, 4, D], BF16)
        bias_lo = sb("bias_lo", [P, 4, D], BF16)
        bias_rest = sb("bias_rest", [P, 4, D])
        bias1 = sb("bias1", [P, T, D], BF16)
        bias2 = sb("bias2", [P, T, D], BF16)
        biasR = sb("biasR", [P, T, 2, D], BF16)
        thirtysecond = sb("thirtysecond", [P, P], BF16)
        identity = sb("identity", [P, P])
        minus_half = sb("minus_half", [P, T])
        eps_1 = sb("eps_1", [P, T])
        eps_4 = sb("eps_4", [P, T])
        minus_one = sb("minus_one", [P, T])

        def slots(name, shape, dtype=FP32):
            return [sb(f"{name}{s}", [P, *shape], dtype) for s in range(SLOTS)]

        xn0 = slots("xn0", [T, D])
        hT = slots("hT", [N])
        qkv = slots("qkv", [2 * N])
        mask = slots("mask", [T, N])
        neg_max = slots("neg_max", [T])
        prob = slots("prob", [T, N])
        prob_sum = slots("prob_sum", [T])
        inv_sum = slots("inv_sum", [T])
        probT = slots("probT", [T, N])
        attn = slots("attn", [T, D])
        th1 = slots("th1", [T, D])
        s1 = slots("s1", [T, D])
        xn1 = slots("xn1", [T, D])
        n1T = slots("n1T", [N])
        th2 = slots("th2", [T, D])
        s2 = slots("s2", [T, D])
        xn2 = slots("xn2", [T, D])
        n2T = slots("n2T", [N])
        lnf = slots("lnf", [T, D])
        xn3 = slots("xn3", [T, D])
        h2T = slots("h2T", [N])
        th3 = slots("th3", [T, D])
        vals = slots("vals", [T, D])
        edges = slots("edges", [T, N])
        result = slots("result", [T, D])
        squares = bias_rest[:, :, :].rearrange("p a d -> p (a d)")
        square_sums = sb("square_sums", [P, G])
        square_max = sb("square_max", [P, 1])
        others_row = sb("others_row", [P, 2], BF16)
        others_flag = sb("others_flag", [1, 2], INT32)
        LN = ("0", "1", "2", "f", "3")
        stats = {n: slots(f"stats{n}", [T, 6]) for n in LN}
        mean_var = {n: slots(f"mean_var{n}", [T, 2]) for n in LN}
        var_eps = {n: slots(f"var_eps{n}", [T]) for n in LN}
        rstd = {n: slots(f"rstd{n}", [T]) for n in LN}
        mean_rstd = {n: slots(f"mean_rstd{n}", [T]) for n in ("1", "2")}
        shift = {n: slots(f"shift{n}", [T]) for n in ("1", "2")}

        def bank(name):
            return ctx.enter_context(nc.psum_tensor(name, [P, 512], FP32))

        ps_qkv = bank("ps_qkv")
        ps_scores = bank("ps_scores")
        ps_attn = bank("ps_attn")
        ps_mlp1 = bank("ps_mlp1")
        ps_mlp2 = bank("ps_mlp2")
        ps_rel = bank("ps_rel")
        ps_t13 = bank("ps_t13")
        ps_t2out = bank("ps_t2out")

        sums = x_all
        table = xn2[0]
        row_number, row_pick = n1T[0][:, 0:P], n2T[0][:, 0:P]
        counters = sb("counters", [P, 2])

        graph_in = [sem(f"graph_in{s}") for s in range(SLOTS)]
        result_out = [sem(f"result_out{s}") for s in range(SLOTS)]
        weights_in = sem("weights_in")
        consts_zeroed = sem("consts_zeroed")
        consts_done = sem("consts_done")
        prep_products = sem("prep_products")
        qkv_weights_ready = sem("qkv_weights_ready")
        prep_copied = sem("prep_copied")
        prep_scaled = sem("prep_scaled")
        prep_products2 = sem("prep_products2")
        rel_gate_ready = sem("rel_gate_ready")
        bias_step = sem("bias_step")
        bias_ready = sem("bias_ready")

        stats_done = {n: sem(f"stats{n}_done") for n in LN}
        mean_var_done = {n: sem(f"mean_var{n}_done") for n in LN}
        eps_added = {n: sem(f"eps_added{n}") for n in LN}
        rstd_done = {n: sem(f"rstd{n}_done") for n in LN}
        mean_scaled = {n: sem(f"mean_scaled{n}") for n in ("1", "2")}
        shift_done = {n: sem(f"shift_done{n}") for n in ("1", "2")}
        norm_done = {n: sem(f"norm{n}_done") for n in LN}
        transposed = {n: sem(f"transposed{n}") for n in ("0", "1", "2", "3")}
        hT_ready = sem("hT_ready")
        qkv_done = sem("qkv_done")
        qkv_ready = sem("qkv_ready")
        mask_ready = sem("mask_ready")
        scores_done = sem("scores_done")
        softmax_in = sem("softmax_in")
        prob_ready = sem("prob_ready")
        probT_done = sem("probT_done")
        probT_ready = sem("probT_ready")
        attn_done = sem("attn_done")
        inv_sum_ready = sem("inv_sum_ready")
        attn_ready = sem("attn_ready")
        tanh1_done = sem("tanh1_done")
        swish1_done = sem("swish1_done")
        n1T_ready = sem("n1T_ready")
        mlp1_done = sem("mlp1_done")
        tanh2_done = sem("tanh2_done")
        swish2_done = sem("swish2_done")
        n2T_ready = sem("n2T_ready")
        mlp2_done = sem("mlp2_done")
        lnfw_done = sem("lnfw_done")
        x_plus_b_ready = sem("x_plus_b_ready")
        x2_ready = sem("x2_ready")
        h2T_ready = sem("h2T_ready")
        rel_done = sem("rel_done")
        tanh3_done = sem("tanh3_done")
        vals_ready = sem("vals_ready")
        edges_selected = sem("edges_selected")
        aggregated = sem("aggregated")
        result_ready = sem("result_ready")
        squares_summed = sem("squares_summed")
        square_max_ready = sem("square_max_ready")
        others_row_ready = sem("others_row_ready")
        others_counted = sem("others_counted")
        flag_ready = sem("flag_ready")
        pass_weights_in = sem("pass_weights_in")
        pass_transposed = sem("pass_transposed")
        pass_copied = sem("pass_copied")
        pass_gated = sem("pass_gated")
        pass_ready = sem("pass_ready")
        table_cleared = sem("table_cleared")
        rows_numbered = sem("rows_numbered")
        node_copied = sem("node_copied")
        node_stats = sem("node_stats")
        node_mean_var = sem("node_mean_var")
        node_eps_added = sem("node_eps_added")
        node_rstd = sem("node_rstd")
        node_normalized = sem("node_normalized")
        node_transposed = sem("node_transposed")
        node_ready = sem("node_ready")
        counters_set = sem("counters_set")
        row_picked = sem("row_picked")
        edges_ready = sem("edges_ready")
        edges_transposed = sem("edges_transposed")
        edges_copied = sem("edges_copied")
        gates_done = sem("gates_done")
        gates_tanh = sem("gates_tanh")
        messages_ready = sem("messages_ready")
        messages_summed = sem("messages_summed")
        sum_added = sem("sum_added")
        sum_halved = sem("sum_halved")
        general_ready = sem("general_ready")
        general_out = sem("general_out")
        waits_taken = sem("waits_taken")

        def run(engine, step):
            for i in range(FIRST_LOOPED):
                step(i, i % SLOTS)
            with engine.Fori(FIRST_LOOPED, G - SLOTS + 1, SLOTS) as i:
                for u in range(SLOTS):
                    step(i + u, u)
            for i in range(G, G + LAST_SKEW + 1):
                step(i, i % SLOTS)

        def stage(name, work, i, u):
            g = i - SKEW[name]
            if not isinstance(i, int) or 0 <= g < G:
                work(g, (u - SKEW[name]) % SLOTS)

        def wait(engine, semaphore, count):
            if not isinstance(count, int):
                engine.wait_ge(semaphore, count)
            elif count > 0:
                engine.wait_ge(semaphore, min(count, G))

        def graph(tensor, g, width):
            return tensor[:, bass.ds(g * width, width)]

        def tiles(ap):
            return ap.rearrange("p (t d) -> p t d", t=T)

        RELATIONS = io["L1_gnn_b_fwd"].shape[0]
        PASSES = (("fwd", 2, RELATIONS, True), ("bwd", 2, RELATIONS, False), ("loop", 1, 1, False))

        def taken(engine, semaphore, count):
            engine.wait_ge(semaphore, count)
            engine.sem_inc(waits_taken, 1)

        def if_others(engine, body):
            engine.wait_ge(flag_ready, 1)
            others = engine.value_load(others_flag[0:1, 0:1], min_val=0, max_val=P)
            with engine.If(others > 0):
                engine.wait_ge(result_ready, G)
                body()

        def over_passes(engine, per_pass, per_graph, per_relation, after_graph=None):
            graphs = relations = 0
            for d, (name, first, number, rows_receive) in enumerate(PASSES):
                if per_pass:
                    per_pass(d, name, first)
                if per_graph or per_relation:
                    with engine.Fori(0, G) as g:
                        k = g + graphs
                        if per_graph:
                            per_graph(g, k, first)
                        if per_relation:
                            with engine.Fori(0, number) as r:
                                per_relation(g, g * number + r + relations, rows_receive)
                        if after_graph:
                            after_graph(d, g)
                graphs += G
                relations += G * number

        block = ctx.enter_context(nc.Block())

        @block.sync
        def _(sp):
            def load(g, s):
                wait(sp, stats_done["0"], g - 1)
                sp.dma_start(graph(x_all, g, W), x_rows[:, bass.ds(g, 1), :].rearrange("p g w -> p (g w)")).then_inc(graph_in[s], 16)
                sp.dma_start(graph(adj_all, g, R), adj_rows[:, bass.ds(g, 1), :].rearrange("p g w -> p (g w)")).then_inc(graph_in[s], 16)

            def store(g, s):
                wait(sp, result_ready, g + 1)
                sp.dma_start(out_rows[:, bass.ds(g, 1), :].rearrange("p g w -> p (g w)"), result[s][:, :, :].rearrange("p t d -> p (t d)")).then_inc(result_out[s], 16)

            for g in range(SLOTS):
                load(g, g)

            def step(i, u):
                if not isinstance(i, int) or i + SLOTS < G:
                    load(i + SLOTS, u)
                stage("result", store, i, u)

            for i in range(FIRST_LOOPED):
                step(i, i % SLOTS)
            with sp.Fori(FIRST_LOOPED, G - 2 * SLOTS + 1, SLOTS) as i:
                for u in range(SLOTS):
                    step(i + u, u)
            for i in range(G - SLOTS, G + LAST_SKEW):
                step(i, i % SLOTS)
            for s in range(SLOTS):
                sp.wait_ge(result_out[s], 16 * (G // SLOTS))

            def general():
                def load_weights(d, name, first):
                    sp.wait_ge(table_cleared, d + 1)
                    number = io[f"L1_gnn_b_{name}"].shape[0]
                    sp.dma_start(Wl[:, :], io[f"L1_gnn_W_{name}"]).then_inc(pass_weights_in, 16)
                    sp.dma_start(Wg[:, :], io[f"L1_gnn_Wg_{name}"]).then_inc(pass_weights_in, 16)
                    sp.dma_start(table[0:number, 0, :], io[f"L1_gnn_b_{name}"]).then_inc(pass_weights_in, 16)
                    sp.dma_start(table[0:number, 1, :], io[f"L1_gnn_bg_{name}"]).then_inc(pass_weights_in, 16)

                over_passes(sp, load_weights, None, None)
                with sp.Fori(0, G) as g:
                    sp.wait_ge(general_ready, g + 1)
                    sp.dma_start(out_rows[:, bass.ds(g, 1), :].rearrange("p g w -> p (g w)"),
                                 result[0][:, :, :].rearrange("p t d -> p (t d)")).then_inc(general_out, 16)
                sp.wait_ge(general_out, 16 * G)

            if_others(sp, general)

        @block.gpsimd
        def _(pool):
            nc.gpsimd.memset(identity[:, :], 0.0).then_inc(consts_zeroed, 1)
            nc.gpsimd.memset(thirtysecond[:, :], 1 / 32).then_inc(consts_done, 1)
            nc.gpsimd.memset(minus_half[:, :], -0.5).then_inc(consts_done, 1)
            nc.gpsimd.memset(eps_1[:, :], EPS).then_inc(consts_done, 1)
            nc.gpsimd.memset(eps_4[:, :], 4 * EPS).then_inc(consts_done, 1)
            nc.gpsimd.memset(minus_one[:, :], -1.0).then_inc(consts_done, 1)
            pool.wait_ge(consts_zeroed, 1)
            nc.gpsimd.affine_select(out=identity[:, :], in_=identity[:, :], compare_op=ALU.not_equal, fill=1.0,
                                    base=0, pattern=[[-1, P]], channel_multiplier=1).then_inc(consts_done, 1)
            pool.wait_ge(consts_done, 6)
            pool.wait_ge(weights_in, 16 * WEIGHT_LOADS)

            def inverse_std(n, eps, g, s):
                wait(pool, mean_var_done[n], g + 1)
                nc.gpsimd.tensor_tensor(var_eps[n][s][:, :], mean_var[n][s][:, :, 1], eps[:, :], ALU.add).then_inc(eps_added[n], 1)
                wait(pool, norm_done[n], g - 1)
                wait(pool, eps_added[n], g + 1)
                nc.gpsimd.tensor_tensor(rstd[n][s][:, :], var_eps[n][s][:, :], minus_half[:, :], ALU.pow).then_inc(rstd_done[n], 1)

            def minus_mean(n, g, s):
                wait(pool, rstd_done[n], g + 1)
                nc.gpsimd.tensor_tensor(mean_rstd[n][s][:, :], mean_var[n][s][:, :, 0], rstd[n][s][:, :], ALU.mult).then_inc(mean_scaled[n], 1)
                wait(pool, mean_scaled[n], g + 1)
                nc.gpsimd.tensor_tensor(shift[n][s][:, :], mean_rstd[n][s][:, :], minus_one[:, :], ALU.mult).then_inc(shift_done[n], 1)

            def rstd0(g, s):
                inverse_std("0", eps_1, g, s)

            def rstd1(g, s):
                inverse_std("1", eps_4, g, s)
                minus_mean("1", g, s)

            def rstd2(g, s):
                inverse_std("2", eps_4, g, s)
                minus_mean("2", g, s)

            def rstdf(g, s):
                inverse_std("f", eps_1, g, s)

            def rstd3(g, s):
                inverse_std("3", eps_1, g, s)

            def add_bias(g, s):
                wait(pool, norm_done["0"], g + 1)
                pool.sem_inc(waits_taken, 1)
                nc.gpsimd.tensor_tensor(tiles(graph(x_all, g, W)), tiles(graph(x_all, g, W)),
                                        lnf_b[:, :].unsqueeze(1).to_broadcast([P, T, D]), ALU.add).then_inc(x_plus_b_ready, 1)

            def scale_f(g, s):
                wait(pool, norm_done["f"], g + 1)
                nc.gpsimd.tensor_tensor(lnf[s][:, :, :], lnf[s][:, :, :], lnf_w[:, :].unsqueeze(1).to_broadcast([P, T, D]),
                                        ALU.mult).then_inc(lnfw_done, 1)

            def step(i, u):
                stage("rstd1", rstd1, i, u)
                stage("rstd2", rstd2, i, u)
                stage("add_bias", add_bias, i, u)
                stage("rstdf", rstdf, i, u)
                stage("rstd0", rstd0, i, u)
                stage("rstd3", rstd3, i, u)
                stage("scale_f", scale_f, i, u)

            run(pool, step)

            def general():
                nc.gpsimd.iota(row_number, pattern=[[0, P]], base=0, channel_multiplier=1,
                               allow_small_or_imprecise_dtypes=True).then_inc(rows_numbered, 1)

                def inverse_std(g, k, first):
                    pool.wait_ge(node_mean_var, k + 1)
                    nc.gpsimd.tensor_tensor(var_eps["3"][0][:, :], mean_var["3"][0][:, :, 1], eps_1[:, :], ALU.add).then_inc(node_eps_added, 1)
                    pool.wait_ge(node_eps_added, k + 1)
                    nc.gpsimd.tensor_tensor(rstd["3"][0][:, :], var_eps["3"][0][:, :], minus_half[:, :], ALU.pow).then_inc(node_rstd, 1)

                over_passes(pool, None, inverse_std, None)

            if_others(pool, general)

        @block.scalar
        def _(act):
            square = ((Wq, "L0_gnn_Wq"), (Wk, "L0_gnn_Wk"), (Wv, "L0_gnn_Wv"), (W1, "L0_gnn_W1"), (W2, "L0_gnn_W2"),
                      (Wl, "L1_gnn_W_loop"), (Wg, "L1_gnn_Wg_loop"))
            for tensor, name in square:
                act.dma_start(tensor[:, :], io[name]).then_inc(weights_in, 16)
            for c, name in enumerate(("L0_gnn_ln1_w", "L0_gnn_ln1_b", "L0_gnn_ln2_w", "L0_gnn_ln2_b")):
                act.dma_start(ln_cols[:, c:c + 1], io[name].unsqueeze(1)).then_inc(weights_in, 16)
            rows = ((bias_rows[:, 0, :], io["L0_gnn_b1"]), (bias_rows[:, 1, :], io["L0_gnn_b2"]),
                    (bias_rows[:, 2, :], io["L1_gnn_b_loop"][0, :]), (bias_rows[:, 3, :], io["L1_gnn_bg_loop"][0, :]),
                    (lnf_w[:, :], io["L0_gnn_lnf_w"]), (lnf_b[:, :], io["L0_gnn_lnf_b"]))
            for to, row in rows:
                act.dma_start(to, row.partition_broadcast(P)).then_inc(weights_in, 16)

            def prepare():
                act.wait_ge(prep_products, 1)
                nc.scalar.activation(QK[:, :], ps_mlp1[:, 0:D], ACT.Copy, scale=1 / math.sqrt(D))
                nc.scalar.activation(WvT[:, :], ps_mlp1[:, D:2 * D], ACT.Copy).then_inc(qkv_weights_ready, 1)
                nc.scalar.activation(W12T[:, :, :], ps_mlp1[:, 2 * D:4 * D].rearrange("p (a d) -> p a d", a=2), ACT.Copy)
                act.wait_ge(prep_products, 2)
                nc.scalar.activation(relW[:, 0, :], ps_mlp2[:, 0:D], ACT.Copy, scale=0.5)
                nc.scalar.activation(WgT[:, :], ps_mlp2[:, D:2 * D], ACT.Copy).then_inc(prep_copied, 1)
                act.wait_ge(prep_products2, 1)
                nc.scalar.activation(relW[:, 1, :], ps_mlp2[:, 0:D], ACT.Copy).then_inc(rel_gate_ready, 1)

            def normalize(n, to, source, g, s):
                wait(act, transposed[n], g - 1)
                wait(act, shift_done[n], g + 1)
                for t in range(T):
                    last = nc.scalar.activation(to[s][:, t, :], source(t), ACT.Identity, bias=shift[n][s][:, t:t + 1],
                                                scale=rstd[n][s][:, t:t + 1])
                last.then_inc(norm_done[n], 1)

            def norm1(g, s):
                normalize("1", xn1, lambda t: s1[s][:, t, :], g, s)

            def norm2(g, s):
                normalize("2", xn2, lambda t: s2[s][:, t, :], g, s)

            def select_edges(g, s):
                wait(act, mask_ready, g + 1)
                wait(act, aggregated, g - 1)
                act.sem_inc(waits_taken, 1)
                nc.scalar.activation(edges[s][:, :, :].rearrange("p t (s q) -> p t s q", s=T),
                                     graph(adj_all, g, R).rearrange("p (t q s) -> p t s q", t=T, s=T), ACT.Copy).then_inc(edges_selected, 1)

            def scale_attn(g, s):
                wait(act, inv_sum_ready, g + 1)
                wait(act, swish1_done, g - 1)
                wait(act, attn_done, g + 1)
                for t in range(T):
                    last = nc.scalar.activation(attn[s][:, t, :], ps_attn[:, t * D:(t + 1) * D], ACT.Copy, scale=inv_sum[s][:, t:t + 1])
                last.then_inc(attn_ready, 1)

            def tanh1(g, s):
                wait(act, attn_ready, g + 1)
                wait(act, swish1_done, g - 1)
                nc.scalar.activation(th1[s][:, :, :], attn[s][:, :, :], ACT.Tanh, scale=0.5).then_inc(tanh1_done, 1)

            def tanh2(g, s):
                wait(act, mlp1_done, g + 1)
                wait(act, swish2_done, g - 1)
                nc.scalar.activation(th2[s][:, :, :], tiles(ps_mlp1[:, 0:W]), ACT.Tanh, scale=0.5).then_inc(tanh2_done, 1)

            def tanh3(g, s):
                wait(act, rel_done, g + 1)
                wait(act, vals_ready, g - 1)
                nc.scalar.activation(th3[s][:, :, :], ps_rel[:, :].rearrange("p (t a d) -> p t a d", t=T, a=2)[:, :, 1, :],
                                     ACT.Tanh, scale=0.5).then_inc(tanh3_done, 1)

            def check(g, s):
                wait(act, mask_ready, g + 1)
                wait(act, squares_summed, g)
                act.sem_inc(waits_taken, 1)
                nc.scalar.activation(squares, graph(adj_all, g, R), ACT.Square, bias=minus_half[:, 0:1],
                                     accum_out=square_sums[:, bass.ds(g, 1)]).then_inc(squares_summed, 1)

            def copy_probT(g, s):
                wait(act, probT_done, g + 1)
                wait(act, attn_done, g - 1)
                nc.scalar.activation(probT[s][:, :, :].rearrange("p t n -> p (t n)"), ps_attn[:, :], ACT.Copy).then_inc(probT_ready, 1)

            def copy_hT(g, s):
                wait(act, transposed["0"], g + 1)
                wait(act, scores_done, g - 1)
                nc.scalar.activation(hT[s][:, :], ps_qkv[:, 0:N], ACT.Relu).then_inc(hT_ready, 1)

            def copy_n1T(g, s):
                wait(act, transposed["1"], g + 1)
                wait(act, mlp1_done, g - 1)
                nc.scalar.activation(n1T[s][:, :], ps_t13[:, 0:N], ACT.Copy).then_inc(n1T_ready, 1)

            def copy_h2T(g, s):
                wait(act, transposed["3"], g + 1)
                wait(act, rel_done, g - 1)
                nc.scalar.activation(h2T[s][:, :], ps_t13[:, 0:N], ACT.Relu).then_inc(h2T_ready, 1)

            def copy_n2T(g, s):
                wait(act, transposed["2"], g + 1)
                wait(act, mlp2_done, g - 1)
                nc.scalar.activation(n2T[s][:, :], ps_t2out[:, 0:N], ACT.Copy).then_inc(n2T_ready, 1)

            def copy_qkv(g, s):
                wait(act, qkv_done, g + 1)
                wait(act, scores_done, g - 1)
                wait(act, attn_done, g - 1)
                nc.scalar.activation(qkv[s][:, :], ps_qkv[:, :], ACT.Copy).then_inc(qkv_ready, 1)

            def exponentials(g, s):
                wait(act, softmax_in, g + 1)
                wait(act, probT_done, g - 1)
                wait(act, inv_sum_ready, g - 1)
                for t in range(T):
                    last = nc.scalar.activation(prob[s][:, t, :], mask[s][:, t, :], ACT.Exp, bias=neg_max[s][:, t:t + 1], scale=-1.0,
                                                accum_out=prob_sum[s][:, t:t + 1])
                last.then_inc(prob_ready, 1)

            prepare()

            def step(i, u):
                stage("tanh2", tanh2, i, u)
                stage("copy_h2T", copy_h2T, i, u)
                stage("tanh1", tanh1, i, u)
                stage("norm1", norm1, i, u)
                stage("norm2", norm2, i, u)
                stage("copy_probT", copy_probT, i, u)
                stage("copy_hT", copy_hT, i, u)
                stage("check", check, i, u)
                stage("copy_n2T", copy_n2T, i, u)
                stage("tanh3", tanh3, i, u)
                stage("copy_n1T", copy_n1T, i, u)
                stage("select_edges", select_edges, i, u)
                stage("exponentials", exponentials, i, u)
                stage("scale_attn", scale_attn, i, u)
                stage("copy_qkv", copy_qkv, i, u)

            run(act, step)

            def general():
                def copy_weights(d, name, first):
                    act.wait_ge(pass_transposed, d + 1)
                    nc.scalar.activation(relW[:, 0, :], ps_scores[:, 0:D], ACT.Copy)
                    nc.scalar.activation(WgT[:, :], ps_scores[:, D:2 * D], ACT.Copy).then_inc(pass_copied, 1)
                    act.wait_ge(pass_gated, d + 1)
                    nc.scalar.activation(relW[:, 1, :], ps_scores[:, 0:D], ACT.Copy).then_inc(pass_ready, 1)

                def copy_nodes(g, k, first):
                    act.wait_ge(node_transposed, k + 1)
                    nc.scalar.activation(h2T[0][:, :], ps_t13[:, 0:N], ACT.Relu).then_inc(node_ready, 1)

                def relation(g, n, rows_receive):
                    if rows_receive:
                        act.wait_ge(edges_transposed, n + 1)
                        nc.scalar.activation(probT[0][:, :, :].rearrange("p t n -> p (t n)"), ps_attn[:, :], ACT.Copy).then_inc(edges_copied, 1)
                    act.wait_ge(gates_done, n + 1)
                    nc.scalar.activation(th3[0][:, :, :], ps_rel[:, :].rearrange("p (t a d) -> p t a d", t=T, a=2)[:, :, 1, :],
                                         ACT.Tanh, scale=0.5).then_inc(gates_tanh, 1)

                over_passes(act, copy_weights, copy_nodes, relation)

            if_others(act, general)

        @block.vector
        def _(dve):
            v = nc.vector
            def prepare():
                dve.wait_ge(weights_in, 16 * WEIGHT_LOADS)
                for a in range(2):
                    last = v.tensor_copy(ln_b_wide[:, a, :], ln_cols[:, 2 * a + 1:2 * a + 2].to_broadcast([P, P]))
                last.then_inc(prep_scaled, 1)
                dve.wait_ge(prep_copied, 1)
                for a in range(2):
                    last = v.tensor_scalar(W12[:, a, :], W12T[:, a, :], ln_cols[:, 2 * a:2 * a + 1], None, ALU.mult)
                last.then_inc(prep_scaled, 1)
                v.tensor_scalar(bias[:, 2, :], bias_rows[:, 2, :], 0.5, None, ALU.mult)
                v.tensor_copy(bias[:, 3, :], bias_rows[:, 3, :])
                dve.wait_ge(prep_products2, 1)
                v.tensor_tensor(bias[:, 0:2, :], ps_rel[:, 0:2 * D].rearrange("p (a d) -> p a d", a=2), bias_rows[:, 0:2, :],
                                ALU.add).then_inc(bias_step, 1)
                dve.wait_ge(bias_step, 1)
                v.tensor_copy(bias_hi[:, :, :], bias[:, :, :]).then_inc(bias_step, 1)
                dve.wait_ge(bias_step, 2)
                v.tensor_tensor(bias_rest[:, :, :], bias[:, :, :], bias_hi[:, :, :], ALU.subtract).then_inc(bias_step, 1)
                dve.wait_ge(bias_step, 3)
                v.tensor_copy(bias_mid[:, :, :], bias_rest[:, :, :]).then_inc(bias_step, 1)
                dve.wait_ge(bias_step, 4)
                v.tensor_tensor(bias_lo[:, :, :], bias_rest[:, :, :], bias_mid[:, :, :], ALU.subtract).then_inc(bias_step, 1)
                dve.wait_ge(bias_step, 5)
                for q, part in enumerate((bias_hi, bias_mid, bias_lo, None)):
                    rows = slice(32 * q, 32 * q + 32)
                    for t in range(T):
                        for to, frm in ((bias1[rows, t, :], 0), (bias2[rows, t, :], 1), (biasR[rows, t, 0, :], 2), (biasR[rows, t, 1, :], 3)):
                            if part is None:
                                last = v.memset(to, 0.0)
                            else:
                                last = v.tensor_copy(to, part[rows, frm, :])
                last.then_inc(bias_ready, 1)

            def statistics(n, source, g, s):
                for t in range(T):
                    last = v.bn_stats(stats[n][s][:, t, :], source(t))
                last.then_inc(stats_done[n], 1)

            def mean_variance(n, g, s):
                wait(dve, norm_done[n], g - 1)
                wait(dve, stats_done[n], g + 1)
                dve.sem_inc(waits_taken, 1)
                for t in range(T):
                    last = v.bn_aggr(mean_var[n][s][:, t, :], stats[n][s][:, t, :])
                last.then_inc(mean_var_done[n], 1)

            def normalize(n, to, source, g, s):
                wait(dve, rstd_done[n], g + 1)
                for t in range(T):
                    last = v.tensor_scalar(to[s][:, t, :], source(t), mean_var[n][s][:, t, 0:1], rstd[n][s][:, t:t + 1],
                                           ALU.subtract, ALU.mult)
                last.then_inc(norm_done[n], 1)

            def stats0(g, s):
                dve.wait_ge(graph_in[s], graphs_in(g, s))
                statistics("0", lambda t: graph(x_all, g * T + t, D), g, s)

            def stats1(g, s):
                wait(dve, swish1_done, g + 1)
                statistics("1", lambda t: s1[s][:, t, :], g, s)

            def stats2(g, s):
                wait(dve, swish2_done, g + 1)
                statistics("2", lambda t: s2[s][:, t, :], g, s)

            def statsf(g, s):
                wait(dve, mlp2_done, g + 1)
                statistics("f", lambda t: ps_mlp2[:, t * D:(t + 1) * D], g, s)

            def stats3(g, s):
                wait(dve, x2_ready, g + 1)
                statistics("3", lambda t: graph(x2_all, g * T + t, D), g, s)

            def mean0(g, s):
                mean_variance("0", g, s)

            def mean1(g, s):
                mean_variance("1", g, s)

            def mean2(g, s):
                mean_variance("2", g, s)

            def meanf(g, s):
                mean_variance("f", g, s)

            def mean3(g, s):
                mean_variance("3", g, s)

            def norm0(g, s):
                wait(dve, transposed["0"], g - 1)
                normalize("0", xn0, lambda t: graph(x_all, g * T + t, D), g, s)

            def norm3(g, s):
                wait(dve, transposed["3"], g - 1)
                normalize("3", xn3, lambda t: graph(x2_all, g * T + t, D), g, s)

            def normf(g, s):
                wait(dve, x2_ready, g - 1)
                normalize("f", lnf, lambda t: ps_mlp2[:, t * D:(t + 1) * D], g, s)

            def make_mask(g, s):
                dve.wait_ge(graph_in[s], graphs_in(g, s))
                wait(dve, prob_ready, g - 1)
                v.tensor_scalar(mask[s][:, :, :].rearrange("p t (s q) -> p t s q", s=T),
                                graph(adj_all, g, R).rearrange("p (t q s) -> p t s q", t=T, s=T),
                                0, MASKED, ALU.is_equal, ALU.mult).then_inc(mask_ready, 1)

            def softmax_input(g, s):
                wait(dve, scores_done, g + 1)
                wait(dve, mask_ready, g + 1)
                dve.sem_inc(waits_taken, 1)
                for t in range(T):
                    last = v.tensor_tensor_reduce(out=mask[s][:, t, :], in0=ps_scores[:, t * N:(t + 1) * N], in1=mask[s][:, t, :],
                                                  scale=-1.0, scalar=3.0e38, op0=ALU.add, op1=ALU.min,
                                                  accum_out=neg_max[s][:, t:t + 1])
                last.then_inc(softmax_in, 1)

            def inverse_sum(g, s):
                wait(dve, prob_ready, g + 1)
                v.reciprocal(inv_sum[s][:, :], prob_sum[s][:, :]).then_inc(inv_sum_ready, 1)

            def swish1(g, s):
                wait(dve, norm_done["1"], g - 1)
                wait(dve, tanh1_done, g + 1)
                v.scalar_tensor_tensor(s1[s][:, :, :], th1[s][:, :, :], 1.0, attn[s][:, :, :], ALU.add, ALU.mult).then_inc(swish1_done, 1)

            def swish2(g, s):
                wait(dve, norm_done["2"], g - 1)
                wait(dve, tanh2_done, g + 1)
                v.scalar_tensor_tensor(s2[s][:, :, :], th2[s][:, :, :], 1.0, tiles(ps_mlp1[:, 0:W]), ALU.add, ALU.mult).then_inc(swish2_done, 1)

            def messages(g, s):
                wait(dve, aggregated, g - 1)
                wait(dve, tanh3_done, g + 1)
                v.scalar_tensor_tensor(vals[s][:, :, :], th3[s][:, :, :], 1.0,
                                       ps_rel[:, :].rearrange("p (t a d) -> p t a d", t=T, a=2)[:, :, 0, :],
                                       ALU.add, ALU.mult).then_inc(vals_ready, 1)

            def residual(g, s):
                wait(dve, x_plus_b_ready, g + 1)
                wait(dve, lnfw_done, g + 1)
                v.tensor_tensor(tiles(graph(x2_all, g, W)), lnf[s][:, :, :], tiles(graph(x_all, g, W)), ALU.add).then_inc(x2_ready, 1)

            def add_messages(g, s):
                if not isinstance(g, int) or g >= SLOTS:
                    dve.wait_ge(result_out[s], results_out(g, s))
                wait(dve, aggregated, g + 1)
                v.scalar_tensor_tensor(result[s][:, :, :], tiles(ps_t2out[:, 0:W]), 0.0, tiles(graph(x2_all, g, W)),
                                       ALU.max, ALU.add).then_inc(result_ready, 1)

            def flag_others():
                dve.wait_ge(squares_summed, G)
                v.reduce_max(square_max[:, :], square_sums[:, :], axis=mybir.AxisListType.X).then_inc(square_max_ready, 1)
                dve.wait_ge(square_max_ready, 1)
                for c in range(2):
                    last = v.tensor_scalar(others_row[:, c:c + 1], square_max[:, :], R / 4 + 1, None, ALU.is_gt)
                last.then_inc(others_row_ready, 1)
                dve.wait_ge(others_counted, 1)
                v.tensor_scalar(others_flag[:, :], ps_scores[0:1, 0:2], 32.0, None, ALU.mult).then_inc(flag_ready, 1)

            def step(i, u):
                if isinstance(i, int) and i == 1:
                    prepare()
                if isinstance(i, int) and i == FLAG_STEP:
                    flag_others()
                stage("messages", messages, i, u)
                stage("stats0", stats0, i, u)
                stage("norm0", norm0, i, u)
                stage("make_mask", make_mask, i, u)
                stage("mean0", mean0, i, u)
                stage("statsf", statsf, i, u)
                stage("residual", residual, i, u)
                stage("meanf", meanf, i, u)
                stage("inverse_sum", inverse_sum, i, u)
                stage("stats3", stats3, i, u)
                stage("swish2", swish2, i, u)
                stage("mean3", mean3, i, u)
                stage("add_messages", add_messages, i, u)
                stage("stats2", stats2, i, u)
                stage("softmax_input", softmax_input, i, u)
                stage("swish1", swish1, i, u)
                stage("normf", normf, i, u)
                stage("stats1", stats1, i, u)
                stage("mean2", mean2, i, u)
                stage("mean1", mean1, i, u)
                stage("norm3", norm3, i, u)

            run(dve, step)

            def general():
                for s in range(SLOTS):
                    dve.wait_ge(result_out[s], 16 * (G // SLOTS))
                dve.wait_ge(rows_numbered, 1)
                v.memset(sums[:, :], 0.0)

                def clear_table(d, name, first):
                    v.memset(table[:, :, :], 0.0).then_inc(table_cleared, 1)

                def normalize_nodes(g, k, first):
                    v.tensor_scalar(s2[0][:, :, :], tiles(graph(x2_all, g, W)), 1.0, None, ALU.mult).then_inc(node_copied, 1)
                    dve.wait_ge(node_copied, k + 1)
                    for t in range(T):
                        last = v.bn_stats(stats["3"][0][:, t, :], s2[0][:, t, :])
                    last.then_inc(node_stats, 1)
                    taken(dve, node_stats, k + 1)
                    for t in range(T):
                        last = v.bn_aggr(mean_var["3"][0][:, t, :], stats["3"][0][:, t, :])
                    last.then_inc(node_mean_var, 1)
                    dve.wait_ge(node_rstd, k + 1)
                    for t in range(T):
                        last = v.tensor_scalar(xn3[0][:, t, :], s2[0][:, t, :], mean_var["3"][0][:, t, 0:1], rstd["3"][0][:, t:t + 1],
                                               ALU.subtract, ALU.mult)
                    last.then_inc(node_normalized, 1)
                    v.memset(counters[:, 0:1], 0.0)
                    v.memset(counters[:, 1:2], float(first)).then_inc(counters_set, 1)
                    taken(dve, counters_set, k + 1)

                def relation(g, n, rows_receive):
                    v.tensor_scalar(row_pick, row_number, counters[:, 0:1], None, ALU.is_equal).then_inc(row_picked, 1)
                    v.tensor_scalar(edges[0][:, :, :].rearrange("p t (s q) -> p t s q", s=T),
                                    graph(adj_all, g, R).rearrange("p (t q s) -> p t s q", t=T, s=T),
                                    counters[:, 1:2], None, ALU.is_equal).then_inc(edges_ready, 1)
                    dve.wait_ge(gates_tanh, n + 1)
                    v.scalar_tensor_tensor(vals[0][:, :, :], th3[0][:, :, :], 1.0,
                                           ps_rel[:, :].rearrange("p (t a d) -> p t a d", t=T, a=2)[:, :, 0, :],
                                           ALU.add, ALU.mult).then_inc(messages_ready, 1)
                    dve.wait_ge(edges_ready, n + 1)
                    v.tensor_scalar(counters[:, :], counters[:, :], 1.0, None, ALU.add)
                    dve.wait_ge(messages_summed, n + 1)
                    v.tensor_tensor(tiles(graph(sums, g, W)), tiles(ps_t2out[:, 0:W]), tiles(graph(sums, g, W)), ALU.add).then_inc(sum_added, 1)
                    taken(dve, sum_added, n + 1)

                def finish(d, g):
                    if d < len(PASSES) - 1:
                        return
                    v.tensor_scalar(s2[0][:, :, :], tiles(graph(sums, g, W)), 0.5, 0.0, ALU.mult, ALU.max).then_inc(sum_halved, 1)
                    dve.wait_ge(sum_halved, g + 1)
                    v.tensor_tensor(result[0][:, :, :], s2[0][:, :, :], tiles(graph(x2_all, g, W)), ALU.add).then_inc(general_ready, 1)
                    dve.wait_ge(general_out, (g + 1) * 16)

                over_passes(dve, clear_table, normalize_nodes, relation, finish)

            if_others(dve, general)

        @block.tensor
        def _(pe):
            mm, transpose = nc.tensor.matmul, nc.tensor.transpose
            def prepare():
                pe.wait_ge(consts_done, 6)
                pe.wait_ge(weights_in, 16 * WEIGHT_LOADS)
                mm(ps_mlp1[:, 0:D], Wq[:, :], Wk[:, :], start=True, stop=True)
                transpose(ps_mlp1[:, D:2 * D], Wv[:, :], identity[:, :])
                transpose(ps_mlp1[:, 2 * D:3 * D], W1[:, :], identity[:, :])
                transpose(ps_mlp1[:, 3 * D:4 * D], W2[:, :], identity[:, :]).then_inc(prep_products, 1)
                transpose(ps_mlp2[:, 0:D], Wl[:, :], identity[:, :])
                transpose(ps_mlp2[:, D:2 * D], Wg[:, :], identity[:, :]).then_inc(prep_products, 1)
                pe.wait_ge(prep_copied, 1)
                pe.wait_ge(prep_scaled, 1)
                for a in range(2):
                    mm(ps_rel[:, a * D:(a + 1) * D], ln_b_wide[:, a, :], W12T[:, a, :], start=True, stop=True)
                mm(ps_mlp2[:, 0:D], Wl[:, :], WgT[:, :], start=True, stop=True).then_inc(prep_products2, 1)
                pe.wait_ge(qkv_weights_ready, 1)

            def prepared():
                pe.wait_ge(prep_scaled, 2)
                pe.wait_ge(rel_gate_ready, 1)
                pe.wait_ge(bias_ready, 1)

            def transpose_rows(bank, source, n):
                for t in range(T):
                    last = transpose(bank[:, t * P:(t + 1) * P], source[:, t, :], identity[:, :])
                last.then_inc(transposed[n], 1)

            def linear(bank, xT, weights, bias_parts, done):
                width = weights.shape[1]
                mm(bank[:, 0:T * width], thirtysecond[:, :], bias_parts, start=True, stop=False, skip_group_check=True)
                for t in range(T):
                    last = mm(bank[:, t * width:(t + 1) * width], xT[:, t * P:(t + 1) * P], weights, start=False, stop=True,
                              skip_group_check=True)
                last.then_inc(done, 1)

            def transpose_probs(g, s):
                wait(pe, attn_ready, g)
                wait(pe, prob_ready, g + 1)
                for c in range(T):
                    for t in range(T):
                        last = transpose(ps_attn[:, c * N + t * P:c * N + (t + 1) * P], prob[s][:, t, c * P:(c + 1) * P], identity[:, :])
                last.then_inc(probT_done, 1)

            def scores(g, s):
                wait(pe, softmax_in, g)
                wait(pe, qkv_ready, g + 1)
                for t in range(T):
                    last = mm(ps_scores[:, t * N:(t + 1) * N], qkv[s][:, t * P:(t + 1) * P], hT[s][:, :], start=True, stop=True)
                last.then_inc(scores_done, 1)

            def transpose0(g, s):
                wait(pe, qkv_ready, g)
                wait(pe, norm_done["0"], g + 1)
                transpose_rows(ps_qkv, xn0[s], "0")

            def transpose1(g, s):
                wait(pe, norm_done["1"], g + 1)
                wait(pe, h2T_ready, g - 4)
                transpose_rows(ps_t13, xn1[s], "1")

            def transpose2(g, s):
                wait(pe, norm_done["2"], g + 1)
                wait(pe, result_ready, g - 3)
                transpose_rows(ps_t2out, xn2[s], "2")

            def transpose3(g, s):
                wait(pe, norm_done["3"], g + 1)
                wait(pe, n1T_ready, g + 5)
                transpose_rows(ps_t13, xn3[s], "3")

            def attend(g, s):
                wait(pe, probT_ready, g + 1)
                for t in range(T):
                    for c in range(T):
                        last = mm(ps_attn[:, t * D:(t + 1) * D], probT[s][:, c, t * P:(t + 1) * P],
                                  qkv[s][:, N + c * D:N + (c + 1) * D], start=(c == 0), stop=(c == T - 1))
                last.then_inc(attn_done, 1)

            def project(g, s):
                wait(pe, hT_ready, g + 1)
                mm(ps_qkv[:, 0:N], QK[:, :], hT[s][:, :], start=True, stop=True)
                for t in range(T):
                    last = mm(ps_qkv[:, N + t * D:N + (t + 1) * D], hT[s][:, t * P:(t + 1) * P], WvT[:, :], start=True, stop=True)
                last.then_inc(qkv_done, 1)

            def mlp1(g, s):
                wait(pe, n1T_ready, g + 1)
                wait(pe, swish2_done, g)
                linear(ps_mlp1, n1T[s], W12[:, 0, :], bias1[:, :, :].rearrange("p t d -> p (t d)"), mlp1_done)

            def mlp2(g, s):
                wait(pe, n2T_ready, g + 1)
                wait(pe, norm_done["f"], g)
                linear(ps_mlp2, n2T[s], W12[:, 1, :], bias2[:, :, :].rearrange("p t d -> p (t d)"), mlp2_done)

            def relate(g, s):
                wait(pe, h2T_ready, g + 1)
                wait(pe, vals_ready, g)
                linear(ps_rel, h2T[s], relW[:, :, :].rearrange("p a d -> p (a d)"),
                       biasR[:, :, :, :].rearrange("p t a d -> p (t a d)"), rel_done)

            def aggregate(g, s):
                wait(pe, vals_ready, g + 1)
                wait(pe, edges_selected, g + 1)
                wait(pe, result_ready, g)
                wait(pe, n2T_ready, g + 4)
                for t in range(T):
                    for c in range(T):
                        last = mm(ps_t2out[:, t * D:(t + 1) * D], edges[s][:, c, t * P:(t + 1) * P], vals[s][:, c, :],
                                  start=(c == 0), stop=(c == T - 1))
                last.then_inc(aggregated, 1)

            prepare()

            def step(i, u):
                if isinstance(i, int) and i == SKEW["mlp1"]:
                    prepared()
                if isinstance(i, int) and i == FLAG_STEP:
                    pe.wait_ge(softmax_in, G)
                    pe.wait_ge(others_row_ready, 1)
                    mm(ps_scores[:, 0:2], thirtysecond[:, :], others_row[:, :], start=True, stop=True).then_inc(others_counted, 1)
                stage("scores", scores, i, u)
                stage("transpose0", transpose0, i, u)
                stage("relate", relate, i, u)
                stage("transpose2", transpose2, i, u)
                stage("transpose1", transpose1, i, u)
                stage("attend", attend, i, u)
                stage("project", project, i, u)
                stage("mlp2", mlp2, i, u)
                stage("mlp1", mlp1, i, u)
                stage("transpose3", transpose3, i, u)
                stage("aggregate", aggregate, i, u)
                stage("transpose_probs", transpose_probs, i, u)

            run(pe, step)

            def general():
                def prepare(d, name, first):
                    pe.wait_ge(pass_weights_in, 16 * 4 * (d + 1))
                    transpose(ps_scores[:, 0:D], Wl[:, :], identity[:, :])
                    transpose(ps_scores[:, D:2 * D], Wg[:, :], identity[:, :]).then_inc(pass_transposed, 1)
                    pe.wait_ge(pass_copied, d + 1)
                    mm(ps_scores[:, 0:D], Wl[:, :], WgT[:, :], start=True, stop=True).then_inc(pass_gated, 1)
                    pe.wait_ge(pass_ready, d + 1)

                def transpose_nodes(g, k, first):
                    pe.wait_ge(node_normalized, k + 1)
                    for t in range(T):
                        last = transpose(ps_t13[:, t * P:(t + 1) * P], xn3[0][:, t, :], identity[:, :])
                    last.then_inc(node_transposed, 1)
                    taken(pe, node_ready, k + 1)

                def relation(g, n, rows_receive):
                    pe.wait_ge(row_picked, n + 1)
                    weights, biases = (a[:, :, :].rearrange("p a d -> p (a d)") for a in (relW, table))
                    for t in range(T):
                        half = ps_rel[:, t * 2 * D:(t + 1) * 2 * D]
                        mm(half, row_pick, biases, start=True, stop=False)
                        last = mm(half, h2T[0][:, t * P:(t + 1) * P], weights, start=False, stop=True)
                    last.then_inc(gates_done, 1)
                    ends = edges[0]
                    pe.wait_ge(edges_ready, n + 1)
                    if rows_receive:
                        for c in range(T):
                            for t in range(T):
                                last = transpose(ps_attn[:, c * N + t * P:c * N + (t + 1) * P], edges[0][:, t, c * P:(c + 1) * P], identity[:, :])
                        last.then_inc(edges_transposed, 1)
                        pe.wait_ge(edges_copied, n + 1)
                        ends = probT[0]
                    pe.wait_ge(messages_ready, n + 1)
                    for t in range(T):
                        for c in range(T):
                            last = mm(ps_t2out[:, t * D:(t + 1) * D], ends[:, c, t * P:(t + 1) * P], vals[0][:, c, :],
                                      start=(c == 0), stop=(c == T - 1))
                    last.then_inc(messages_summed, 1)

                over_passes(pe, prepare, transpose_nodes, relation)

            if_others(pe, general)


WEIGHT_LOADS = 17


def graphs_in(g, s):
    return 16 * 2 * (g // SLOTS + 1) if isinstance(g, int) else (g - s) * (16 * 2 // SLOTS) + 16 * 2


def results_out(g, s):
    return 16 * (g // SLOTS) if isinstance(g, int) else (g - s) * (16 // SLOTS)


_INS = ["x", "adj", "L0_gnn_Wq", "L0_gnn_Wk", "L0_gnn_Wv", "L0_gnn_ln1_w", "L0_gnn_ln1_b", "L0_gnn_W1", "L0_gnn_b1",
        "L0_gnn_ln2_w", "L0_gnn_ln2_b", "L0_gnn_W2", "L0_gnn_b2", "L0_gnn_lnf_w", "L0_gnn_lnf_b",
        *(f"L1_gnn_{kind}_{name}" for kind in ("W", "Wg", "b", "bg") for name in ("fwd", "bwd", "loop"))]


def kernel(**inputs):
    import numpy as np
    import concourse.bacc as bacc
    from concourse.bass_utils import run_bass_kernel_spmd

    nc = bacc.Bacc("TRN2", target_bir_lowering=False, num_devices=1)
    arrays, io = {}, {}
    for name in _INS:
        a = np.ascontiguousarray(inputs[name])
        arrays[f"in_{name}"] = a
        io[name] = nc.dram_tensor(f"in_{name}", a.shape, mybir.dt.from_np(a.dtype), kind="ExternalInput").ap()
    out = nc.dram_tensor("out", arrays["in_x"].shape, FP32, kind="ExternalOutput").ap()
    graph_layers(nc, io, out)
    r = run_bass_kernel_spmd(nc, [arrays], core_ids=[0])
    return r.results[0]["out"]
```

```python
import math
from contextlib import ExitStack

import concourse.bass as bass
from concourse import mybir

FP32 = mybir.dt.float32
BF16 = mybir.dt.bfloat16
INT32 = mybir.dt.int32
ALU = mybir.AluOpType
ACT = mybir.ActivationFunctionType

P = 128
EPS = 1e-5
MASKED = -1000000000.0
SLOTS = 2


def graph_layers(nc, io, out):
    x, adj = io["x"], io["adj"]
    G, N, D = x.shape
    T = N // P
    W = T * D
    R = T * N

    x_rows = x.rearrange("g (p t) d -> p g (t d)", t=T)
    adj_rows = adj.rearrange("g (p t) n -> p g (t n)", t=T)
    out_rows = out.rearrange("g (p t) d -> p g (t d)", t=T)

    STAGES = dict(
        sp=dict(
            load_x=0, load_adj=3, store=14),
        pool=dict(
            eps1=6, rstdf=9, eps3=10, rstd1=6, rstd3=10, norm1=6, rstd0=1, eps2=7, residual=9,
            add_bias=2, rstd2=7, eps0=0, norm2=7, epsf=8),
        act=dict(
            copy_n1T=5, copy_qkv=2, select_edges=10, copy_probT=3, tanh2=5, copy_hT=1, copy_h2T=9,
            norm0=0, check=9, scale_attn=3, copy_n2T=6, tanh1=3, exponentials=2, tanh3=9),
        dve=dict(
            normf=9, mean2=7, softmax_input=4, norm3=10, make_mask=3, stats0=0, shift0=1, swish1=5,
            mean0=0, statsf=8, stats1=5, inverse_sum=4, meanf=8, mean1=5, stats3=9, messages=11, mean3=9,
            add_messages=12, swish2=6, stats2=6),
        pe=dict(
            transpose2=6, project=1, relate=9, mlp2=6, transpose1=4, aggregate=10, transpose_probs=2,
            mlp1=4, transpose0=0, transpose3=8, scores=1, attend=2),
    )
    SKEW = {name: skew for stages in STAGES.values() for name, skew in stages.items()}

    ctx = ExitStack()
    with ctx:
        def sb(name, shape, dtype=FP32):
            return ctx.enter_context(nc.sbuf_tensor(name, shape, dtype))

        def sem(name):
            return ctx.enter_context(nc.semaphore(name))

        x_all = sb("x_all", [P, G * W])
        x2_all = sb("x2_all", [P, G * W])
        adj_all = sb("adj_all", [P, G * R], INT32)

        square = sb("square", [P, len(SQUARE), D])
        Wq, Wk, WvT, W1T, W2, WlT, WgT, Wl = (square[:, k, :] for k in range(len(SQUARE)))
        Wg = sb("Wg", [P, D])
        columns = sb("columns", [P, len(COLUMNS)])
        rows = sb("rows", [P, len(ROWS), D])
        lnf_w, lnf_b = rows[:, 2, :], rows[:, 3, :]

        QK = sb("QK", [P, D])
        W12T = sb("W12T", [P, 2, D])
        W12s = sb("W12s", [P, 2, D])
        W12 = sb("W12", [P, 2, D])
        relW = sb("relW", [P, 2, D])
        wide = sb("wide", [P, 4, P])
        bias = sb("bias", [P, 4, D])
        bias_rest = sb("bias_rest", [P, 4, D])
        bias_mid = sb("bias_mid", [P, 4, D], BF16)
        bias_parts = sb("bias_parts", [P, 4, D], BF16)
        thirtysecond = sb("thirtysecond", [P, P], BF16)
        identity = sb("identity", [P, P])
        centering = sb("centering", [P, P])
        minus_half = sb("minus_half", [P, T])
        eps_1 = sb("eps_1", [P, T])
        eps_4 = sb("eps_4", [P, T])

        def slots(name, shape, dtype=FP32):
            return [sb(f"{name}{s}", [P, *shape], dtype) for s in range(SLOTS)]

        xn0 = slots("xn0", [T, D])
        hT = slots("hT", [N])
        qkv = slots("qkv", [2 * N])
        mask = slots("mask", [T, N])
        neg_max = slots("neg_max", [T])
        prob = slots("prob", [T, N])
        prob_sum = slots("prob_sum", [T])
        inv_sum = slots("inv_sum", [T])
        probT = slots("probT", [T, N])
        attn = slots("attn", [T, D])
        th1 = slots("th1", [T, D])
        s1 = slots("s1", [T, D])
        xn1 = slots("xn1", [T, D])
        n1T = slots("n1T", [N])
        th2 = slots("th2", [T, D])
        s2 = slots("s2", [T, D])
        xn2 = slots("xn2", [T, D])
        n2T = slots("n2T", [N])
        lnf = slots("lnf", [T, D])
        xn3 = slots("xn3", [T, D])
        h2T = slots("h2T", [N])
        th3 = slots("th3", [T, D])
        vals = slots("vals", [T, D])
        edges = slots("edges", [T, N])
        result = slots("result", [T, D])
        squares = bias_rest[:, :, :].rearrange("p a d -> p (a d)")
        square_sums = sb("square_sums", [P, G])
        square_max = sb("square_max", [P, 1])
        others_row = sb("others_row", [P, 2], BF16)
        others_flag = sb("others_flag", [1, 2], INT32)
        LN = ("0", "1", "2", "f", "3")
        stats = {n: slots(f"stats{n}", [T, 6]) for n in LN}
        mean_var = {n: slots(f"mean_var{n}", [T, 2]) for n in LN}
        var_eps = {n: slots(f"var_eps{n}", [T]) for n in LN}
        rstd = {n: slots(f"rstd{n}", [T]) for n in LN}
        shift = slots("shift", [T])

        def bank(name):
            return ctx.enter_context(nc.psum_tensor(name, [P, 512], FP32))

        ps_qkv = bank("ps_qkv")
        ps_scores = bank("ps_scores")
        ps_attn = bank("ps_attn")
        ps_mlp1 = bank("ps_mlp1")
        ps_mlp2 = bank("ps_mlp2")
        ps_rel = bank("ps_rel")
        ps_t13 = bank("ps_t13")
        ps_t2out = bank("ps_t2out")

        sums = x_all
        table = xn2[0]
        row_number, row_pick = n1T[0][:, 0:P], n2T[0][:, 0:P]
        counters = sb("counters", [P, 2])

        x_in = [sem(f"x_in{s}") for s in range(SLOTS)]
        adj_in = [sem(f"adj_in{s}") for s in range(SLOTS)]
        result_out = [sem(f"result_out{s}") for s in range(SLOTS)]
        qkv_weights_in = sem("qkv_weights_in")
        weights_in = sem("weights_in")
        consts_zeroed = sem("consts_zeroed")
        consts_done = sem("consts_done")
        qk_product = sem("qk_product")
        qk_ready = sem("qk_ready")
        w2_centered = sem("w2_centered")
        mlp_scaled = sem("mlp_scaled")
        mlp_centered = sem("mlp_centered")
        mlp_ready = sem("mlp_ready")
        rel_gate_product = sem("rel_gate_product")
        rel_gate_ready = sem("rel_gate_ready")
        bias_step = sem("bias_step")
        bias_ready = sem("bias_ready")

        stats_done = {n: sem(f"stats{n}_done") for n in LN}
        mean_var_done = {n: sem(f"mean_var{n}_done") for n in LN}
        eps_added = {n: sem(f"eps_added{n}") for n in LN}
        rstd_done = {n: sem(f"rstd{n}_done") for n in LN}
        shift_done = sem("shift_done")
        norm_done = {n: sem(f"norm{n}_done") for n in LN}
        transposed = {n: sem(f"transposed{n}") for n in ("0", "1", "2", "3")}
        hT_ready = sem("hT_ready")
        qkv_done = sem("qkv_done")
        qkv_ready = sem("qkv_ready")
        mask_ready = sem("mask_ready")
        scores_done = sem("scores_done")
        softmax_in = sem("softmax_in")
        prob_ready = sem("prob_ready")
        probT_done = sem("probT_done")
        probT_ready = sem("probT_ready")
        attn_done = sem("attn_done")
        inv_sum_ready = sem("inv_sum_ready")
        attn_ready = sem("attn_ready")
        tanh1_done = sem("tanh1_done")
        swish1_done = sem("swish1_done")
        n1T_ready = sem("n1T_ready")
        mlp1_done = sem("mlp1_done")
        tanh2_done = sem("tanh2_done")
        swish2_done = sem("swish2_done")
        n2T_ready = sem("n2T_ready")
        mlp2_done = sem("mlp2_done")
        x_plus_b_ready = sem("x_plus_b_ready")
        x2_ready = sem("x2_ready")
        h2T_ready = sem("h2T_ready")
        rel_done = sem("rel_done")
        tanh3_done = sem("tanh3_done")
        vals_ready = sem("vals_ready")
        edges_selected = sem("edges_selected")
        aggregated = sem("aggregated")
        result_ready = sem("result_ready")
        squares_summed = sem("squares_summed")
        square_max_ready = sem("square_max_ready")
        others_row_ready = sem("others_row_ready")
        others_counted = sem("others_counted")
        flag_ready = sem("flag_ready")
        pass_weights_in = sem("pass_weights_in")
        pass_transposed = sem("pass_transposed")
        pass_copied = sem("pass_copied")
        pass_gated = sem("pass_gated")
        pass_ready = sem("pass_ready")
        table_cleared = sem("table_cleared")
        rows_numbered = sem("rows_numbered")
        node_copied = sem("node_copied")
        node_stats = sem("node_stats")
        node_mean_var = sem("node_mean_var")
        node_eps_added = sem("node_eps_added")
        node_rstd = sem("node_rstd")
        node_normalized = sem("node_normalized")
        node_transposed = sem("node_transposed")
        node_ready = sem("node_ready")
        counters_set = sem("counters_set")
        row_picked = sem("row_picked")
        edges_ready = sem("edges_ready")
        edges_transposed = sem("edges_transposed")
        edges_copied = sem("edges_copied")
        gates_done = sem("gates_done")
        gates_tanh = sem("gates_tanh")
        messages_ready = sem("messages_ready")
        messages_summed = sem("messages_summed")
        sum_added = sem("sum_added")
        sum_halved = sem("sum_halved")
        general_ready = sem("general_ready")
        general_out = sem("general_out")
        waits_taken = sem("waits_taken")

        def run(engine, step, stages):
            first_looped = -(-(max(stages.values()) + SLOTS) // SLOTS) * SLOTS
            for i in range(first_looped):
                step(i, i % SLOTS)
            with engine.Fori(first_looped, G - SLOTS + 1, SLOTS) as i:
                for u in range(SLOTS):
                    step(i + u, u)
            for i in range(G, G + max(stages.values())):
                step(i, i % SLOTS)

        def stage(name, work, i, u):
            g = i - SKEW[name]
            if not isinstance(i, int) or 0 <= g < G:
                work(g, (u - SKEW[name]) % SLOTS)

        def first(name, i):
            return isinstance(i, int) and i == SKEW[name]

        def wait(engine, semaphore, count):
            if not isinstance(count, int):
                engine.wait_ge(semaphore, count)
            elif count > 0:
                engine.wait_ge(semaphore, min(count, G))

        def graph(tensor, g, width):
            return tensor[:, bass.ds(g * width, width)]

        def tiles(ap):
            return ap.rearrange("p (t d) -> p t d", t=T)

        RELATIONS = io["L1_gnn_b_fwd"].shape[0]
        PASSES = (("fwd", 2, RELATIONS, True), ("bwd", 2, RELATIONS, False), ("loop", 1, 1, False))

        def taken(engine, semaphore, count):
            engine.wait_ge(semaphore, count)
            engine.sem_inc(waits_taken, 1)

        def if_others(engine, body):
            engine.wait_ge(flag_ready, 1)
            others = engine.value_load(others_flag[0:1, 0:1], min_val=0, max_val=P)
            with engine.If(others > 0):
                engine.wait_ge(result_ready, G)
                body()

        def over_passes(engine, per_pass, per_graph, per_relation, after_graph=None):
            graphs = relations = 0
            for d, (name, first, number, rows_receive) in enumerate(PASSES):
                if per_pass:
                    per_pass(d, name, first)
                if per_graph or per_relation:
                    with engine.Fori(0, G) as g:
                        k = g + graphs
                        if per_graph:
                            per_graph(g, k, first)
                        if per_relation:
                            with engine.Fori(0, number) as r:
                                per_relation(g, g * number + r + relations, rows_receive)
                        if after_graph:
                            after_graph(d, g)
                graphs += G
                relations += G * number

        block = ctx.enter_context(nc.Block())

        @block.sync
        def _(sp):
            def load_x(g, s):
                wait(sp, stats_done["0"], g - 1)
                sp.dma_start(graph(x_all, g, W), x_rows[:, bass.ds(g, 1), :].rearrange("p g w -> p (g w)")).then_inc(x_in[s], 16)

            def load_adj(g, s):
                wait(sp, mask_ready, g - 1)
                sp.dma_start(graph(adj_all, g, R), adj_rows[:, bass.ds(g, 1), :].rearrange("p g w -> p (g w)")).then_inc(adj_in[s], 16)

            def store(g, s):
                wait(sp, result_ready, g + 1)
                sp.dma_start(out_rows[:, bass.ds(g, 1), :].rearrange("p g w -> p (g w)"), result[s][:, :, :].rearrange("p t d -> p (t d)")).then_inc(result_out[s], 16)

            def step(i, u):
                stage("load_x", load_x, i, u)
                stage("load_adj", load_adj, i, u)
                stage("store", store, i, u)

            run(sp, step, STAGES["sp"])

            for s in range(SLOTS):
                sp.wait_ge(result_out[s], 16 * (G // SLOTS))

            def general():
                def load_weights(d, name, first):
                    sp.wait_ge(table_cleared, d + 1)
                    number = io[f"L1_gnn_b_{name}"].shape[0]
                    sp.dma_start(Wl, io[f"L1_gnn_W_{name}"]).then_inc(pass_weights_in, 16)
                    sp.dma_start(Wg[:, :], io[f"L1_gnn_Wg_{name}"]).then_inc(pass_weights_in, 16)
                    sp.dma_start(table[0:number, 0, :], io[f"L1_gnn_b_{name}"]).then_inc(pass_weights_in, 16)
                    sp.dma_start(table[0:number, 1, :], io[f"L1_gnn_bg_{name}"]).then_inc(pass_weights_in, 16)

                over_passes(sp, load_weights, None, None)
                with sp.Fori(0, G) as g:
                    sp.wait_ge(general_ready, g + 1)
                    sp.dma_start(out_rows[:, bass.ds(g, 1), :].rearrange("p g w -> p (g w)"),
                                 result[0][:, :, :].rearrange("p t d -> p (t d)")).then_inc(general_out, 16)
                sp.wait_ge(general_out, 16 * G)

            if_others(sp, general)

        @block.gpsimd
        def _(pool):
            nc.gpsimd.memset(identity[:, :], 0.0).then_inc(consts_zeroed, 1)
            nc.gpsimd.memset(thirtysecond[:, :], 1 / 32).then_inc(consts_done, 1)
            nc.gpsimd.memset(minus_half[:, :], -0.5).then_inc(consts_done, 1)
            nc.gpsimd.memset(eps_1[:, :], EPS).then_inc(consts_done, 1)
            nc.gpsimd.memset(eps_4[:, :], 4 * EPS).then_inc(consts_done, 1)
            nc.gpsimd.memset(centering[:, :], -1 / D).then_inc(consts_zeroed, 1)
            pool.wait_ge(consts_zeroed, 2)
            nc.gpsimd.affine_select(out=identity[:, :], in_=identity[:, :], compare_op=ALU.not_equal, fill=1.0,
                                    base=0, pattern=[[-1, P]], channel_multiplier=1).then_inc(consts_done, 1)
            nc.gpsimd.affine_select(out=centering[:, :], in_=centering[:, :], compare_op=ALU.not_equal, fill=1 - 1 / D,
                                    base=0, pattern=[[-1, P]], channel_multiplier=1).then_inc(consts_done, 1)

            def add_eps(n, eps, g, s):
                wait(pool, rstd_done[n], g - 1)
                wait(pool, mean_var_done[n], g + 1)
                nc.gpsimd.tensor_tensor(var_eps[n][s][:, :], mean_var[n][s][:, :, 1], eps[:, :], ALU.add).then_inc(eps_added[n], 1)

            def inverse_std(n, g, s):
                wait(pool, norm_done[n], g - 1)
                wait(pool, eps_added[n], g + 1)
                nc.gpsimd.tensor_tensor(rstd[n][s][:, :], var_eps[n][s][:, :], minus_half[:, :], ALU.pow).then_inc(rstd_done[n], 1)

            def scale_rows(n, to, source, g, s):
                wait(pool, transposed[n], g - 1)
                wait(pool, rstd_done[n], g + 1)
                nc.gpsimd.tensor_tensor(to[s][:, :, :], source[s][:, :, :], rstd[n][s][:, :].unsqueeze(2).to_broadcast([P, T, D]),
                                        ALU.mult).then_inc(norm_done[n], 1)

            def eps0(g, s):
                add_eps("0", eps_1, g, s)

            def eps1(g, s):
                add_eps("1", eps_4, g, s)

            def eps2(g, s):
                add_eps("2", eps_4, g, s)

            def epsf(g, s):
                add_eps("f", eps_1, g, s)

            def eps3(g, s):
                add_eps("3", eps_1, g, s)

            def rstd0(g, s):
                inverse_std("0", g, s)

            def rstd1(g, s):
                inverse_std("1", g, s)

            def rstd2(g, s):
                inverse_std("2", g, s)

            def rstdf(g, s):
                inverse_std("f", g, s)

            def rstd3(g, s):
                inverse_std("3", g, s)

            def norm1(g, s):
                scale_rows("1", xn1, s1, g, s)

            def norm2(g, s):
                scale_rows("2", xn2, s2, g, s)

            def add_bias(g, s):
                wait(pool, norm_done["0"], g + 1)
                pool.sem_inc(waits_taken, 1)
                nc.gpsimd.tensor_tensor(tiles(graph(x_all, g, W)), tiles(graph(x_all, g, W)),
                                        lnf_b.unsqueeze(1).to_broadcast([P, T, D]), ALU.add).then_inc(x_plus_b_ready, 1)

            def residual(g, s):
                wait(pool, x_plus_b_ready, g + 1)
                wait(pool, norm_done["f"], g + 1)
                pool.sem_inc(waits_taken, 1)
                nc.gpsimd.tensor_tensor(tiles(graph(x2_all, g, W)), lnf[s][:, :, :], tiles(graph(x_all, g, W)), ALU.add).then_inc(x2_ready, 1)

            def step(i, u):
                if first("add_bias", i):
                    pool.wait_ge(weights_in, 16 * WEIGHT_LOADS)
                stage("eps1", eps1, i, u)
                stage("rstdf", rstdf, i, u)
                stage("eps3", eps3, i, u)
                stage("rstd1", rstd1, i, u)
                stage("rstd3", rstd3, i, u)
                stage("norm1", norm1, i, u)
                stage("rstd0", rstd0, i, u)
                stage("eps2", eps2, i, u)
                stage("residual", residual, i, u)
                stage("add_bias", add_bias, i, u)
                stage("rstd2", rstd2, i, u)
                stage("eps0", eps0, i, u)
                stage("norm2", norm2, i, u)
                stage("epsf", epsf, i, u)

            run(pool, step, STAGES["pool"])

            def general():
                nc.gpsimd.iota(row_number, pattern=[[0, P]], base=0, channel_multiplier=1,
                               allow_small_or_imprecise_dtypes=True).then_inc(rows_numbered, 1)

                def inverse_std(g, k, first):
                    pool.wait_ge(node_mean_var, k + 1)
                    nc.gpsimd.tensor_tensor(var_eps["3"][0][:, :], mean_var["3"][0][:, :, 1], eps_1[:, :], ALU.add).then_inc(node_eps_added, 1)
                    pool.wait_ge(node_eps_added, k + 1)
                    nc.gpsimd.tensor_tensor(rstd["3"][0][:, :], var_eps["3"][0][:, :], minus_half[:, :], ALU.pow).then_inc(node_rstd, 1)

                over_passes(pool, None, inverse_std, None)

            if_others(pool, general)

        @block.scalar
        def _(act):
            act.dma_start(square[:, 0:3, :], io["square"][:, 0:3, :]).then_inc(qkv_weights_in, 16)
            act.dma_start(square[:, 3:len(SQUARE), :], io["square"][:, 3:len(SQUARE), :]).then_inc(weights_in, 16)
            act.dma_start(columns[:, :], io["columns"]).then_inc(weights_in, 16)
            act.dma_start(rows[:, :, :].rearrange("p a d -> p (a d)"), io["rows"].partition_broadcast(P)).then_inc(weights_in, 16)

            def prepare_qk():
                act.wait_ge(qk_product, 1)
                nc.scalar.activation(QK[:, :], ps_mlp1[:, 0:D], ACT.Copy, scale=1 / math.sqrt(D)).then_inc(qk_ready, 1)

            def prepare_rest():
                act.wait_ge(mlp_centered, 1)
                nc.scalar.activation(bias[:, 2, :], rows[:, 0, :], ACT.Copy, scale=0.5)
                nc.scalar.activation(bias[:, 3, :], rows[:, 1, :], ACT.Copy)
                nc.scalar.activation(bias[:, 0:2, :].rearrange("p a d -> p (a d)"), ps_rel[:, 0:2 * D], ACT.Copy).then_inc(bias_step, 1)
                nc.scalar.activation(W12[:, :, :].rearrange("p a d -> p (a d)"), ps_mlp2[:, 0:2 * D], ACT.Copy).then_inc(mlp_ready, 1)
                act.wait_ge(rel_gate_product, 1)
                nc.scalar.activation(relW[:, 0, :], WlT, ACT.Copy, scale=0.5)
                nc.scalar.activation(relW[:, 1, :], ps_mlp1[:, 0:D], ACT.Copy).then_inc(rel_gate_ready, 1)

            def norm0(g, s):
                wait(act, transposed["0"], g - 1)
                wait(act, shift_done, g + 1)
                act.sem_inc(waits_taken, 1)
                for t in range(T):
                    last = nc.scalar.activation(xn0[s][:, t, :], graph(x_all, g * T + t, D), ACT.Identity,
                                                bias=shift[s][:, t:t + 1], scale=rstd["0"][s][:, t:t + 1])
                last.then_inc(norm_done["0"], 1)

            def select_edges(g, s):
                wait(act, mask_ready, g + 1)
                wait(act, aggregated, g - 1)
                act.sem_inc(waits_taken, 1)
                nc.scalar.activation(edges[s][:, :, :].rearrange("p t (s q) -> p t s q", s=T),
                                     graph(adj_all, g, R).rearrange("p (t q s) -> p t s q", t=T, s=T), ACT.Copy).then_inc(edges_selected, 1)

            def scale_attn(g, s):
                wait(act, inv_sum_ready, g + 1)
                wait(act, swish1_done, g - 1)
                wait(act, attn_done, g + 1)
                for t in range(T):
                    last = nc.scalar.activation(attn[s][:, t, :], ps_attn[:, t * D:(t + 1) * D], ACT.Copy, scale=inv_sum[s][:, t:t + 1])
                last.then_inc(attn_ready, 1)

            def tanh1(g, s):
                wait(act, attn_ready, g + 1)
                wait(act, swish1_done, g - 1)
                nc.scalar.activation(th1[s][:, :, :], attn[s][:, :, :], ACT.Tanh, scale=0.5).then_inc(tanh1_done, 1)

            def tanh2(g, s):
                wait(act, mlp1_done, g + 1)
                wait(act, swish2_done, g - 1)
                nc.scalar.activation(th2[s][:, :, :], tiles(ps_mlp1[:, 0:W]), ACT.Tanh, scale=0.5).then_inc(tanh2_done, 1)

            def tanh3(g, s):
                wait(act, rel_done, g + 1)
                wait(act, vals_ready, g - 1)
                nc.scalar.activation(th3[s][:, :, :], ps_rel[:, :].rearrange("p (t a d) -> p t a d", t=T, a=2)[:, :, 1, :],
                                     ACT.Tanh, scale=0.5).then_inc(tanh3_done, 1)

            def check(g, s):
                wait(act, mask_ready, g + 1)
                wait(act, squares_summed, g)
                act.sem_inc(waits_taken, 1)
                nc.scalar.activation(squares, graph(adj_all, g, R), ACT.Square, bias=minus_half[:, 0:1],
                                     accum_out=square_sums[:, bass.ds(g, 1)]).then_inc(squares_summed, 1)

            def copy_probT(g, s):
                wait(act, probT_done, g + 1)
                wait(act, attn_done, g - 1)
                nc.scalar.activation(probT[s][:, :, :].rearrange("p t n -> p (t n)"), ps_attn[:, :], ACT.Copy).then_inc(probT_ready, 1)

            def copy_hT(g, s):
                wait(act, transposed["0"], g + 1)
                wait(act, scores_done, g - 1)
                nc.scalar.activation(hT[s][:, :], ps_qkv[:, 0:N], ACT.Relu).then_inc(hT_ready, 1)

            def copy_n1T(g, s):
                wait(act, transposed["1"], g + 1)
                wait(act, mlp1_done, g - 1)
                nc.scalar.activation(n1T[s][:, :], ps_t13[:, 0:N], ACT.Copy).then_inc(n1T_ready, 1)

            def copy_h2T(g, s):
                wait(act, transposed["3"], g + 1)
                wait(act, rel_done, g - 1)
                nc.scalar.activation(h2T[s][:, :], ps_t13[:, 0:N], ACT.Relu).then_inc(h2T_ready, 1)

            def copy_n2T(g, s):
                wait(act, transposed["2"], g + 1)
                wait(act, mlp2_done, g - 1)
                nc.scalar.activation(n2T[s][:, :], ps_t2out[:, 0:N], ACT.Copy).then_inc(n2T_ready, 1)

            def copy_qkv(g, s):
                wait(act, qkv_done, g + 1)
                wait(act, scores_done, g - 1)
                wait(act, attn_done, g - 1)
                nc.scalar.activation(qkv[s][:, :], ps_qkv[:, :], ACT.Copy).then_inc(qkv_ready, 1)

            def exponentials(g, s):
                wait(act, softmax_in, g + 1)
                wait(act, probT_done, g - 1)
                wait(act, inv_sum_ready, g - 1)
                for t in range(T):
                    last = nc.scalar.activation(prob[s][:, t, :], mask[s][:, t, :], ACT.Exp, bias=neg_max[s][:, t:t + 1], scale=-1.0,
                                                accum_out=prob_sum[s][:, t:t + 1])
                last.then_inc(prob_ready, 1)

            prepare_qk()

            def step(i, u):
                stage("copy_n1T", copy_n1T, i, u)
                stage("copy_qkv", copy_qkv, i, u)
                stage("select_edges", select_edges, i, u)
                stage("copy_probT", copy_probT, i, u)
                stage("tanh2", tanh2, i, u)
                stage("copy_hT", copy_hT, i, u)
                stage("copy_h2T", copy_h2T, i, u)
                stage("norm0", norm0, i, u)
                stage("check", check, i, u)
                stage("scale_attn", scale_attn, i, u)
                stage("copy_n2T", copy_n2T, i, u)
                stage("tanh1", tanh1, i, u)
                stage("exponentials", exponentials, i, u)
                if first("exponentials", i):
                    prepare_rest()
                stage("tanh3", tanh3, i, u)

            run(act, step, STAGES["act"])

            def general():
                def copy_weights(d, name, first):
                    act.wait_ge(pass_transposed, d + 1)
                    nc.scalar.activation(relW[:, 0, :], ps_scores[:, 0:D], ACT.Copy)
                    nc.scalar.activation(WgT, ps_scores[:, D:2 * D], ACT.Copy).then_inc(pass_copied, 1)
                    act.wait_ge(pass_gated, d + 1)
                    nc.scalar.activation(relW[:, 1, :], ps_scores[:, 0:D], ACT.Copy).then_inc(pass_ready, 1)

                def copy_nodes(g, k, first):
                    act.wait_ge(node_transposed, k + 1)
                    nc.scalar.activation(h2T[0][:, :], ps_t13[:, 0:N], ACT.Relu).then_inc(node_ready, 1)

                def relation(g, n, rows_receive):
                    if rows_receive:
                        act.wait_ge(edges_transposed, n + 1)
                        nc.scalar.activation(probT[0][:, :, :].rearrange("p t n -> p (t n)"), ps_attn[:, :], ACT.Copy).then_inc(edges_copied, 1)
                    act.wait_ge(gates_done, n + 1)
                    nc.scalar.activation(th3[0][:, :, :], ps_rel[:, :].rearrange("p (t a d) -> p t a d", t=T, a=2)[:, :, 1, :],
                                         ACT.Tanh, scale=0.5).then_inc(gates_tanh, 1)

                over_passes(act, copy_weights, copy_nodes, relation)

            if_others(act, general)

        @block.vector
        def _(dve):
            v = nc.vector
            def prepare_mlp():
                dve.wait_ge(weights_in, 16 * WEIGHT_LOADS)
                for a in range(4):
                    v.tensor_copy(wide[:, a, :], columns[:, a:a + 1].to_broadcast([P, P]))
                v.tensor_copy(W12T[:, 0, :], W1T)
                v.tensor_scalar(W12s[:, 0, :], W1T, columns[:, 4:5], None, ALU.mult)
                dve.wait_ge(w2_centered, 1)
                v.tensor_copy(W12T[:, 1, :], ps_mlp2[:, 0:D])
                v.tensor_scalar(W12s[:, 1, :], ps_mlp2[:, 0:D], columns[:, 5:6], None, ALU.mult).then_inc(mlp_scaled, 1)

            def split_biases():
                dve.wait_ge(bias_step, 1)
                v.tensor_copy(bias_parts[:, :, :], bias[:, :, :]).then_inc(bias_step, 1)
                dve.wait_ge(bias_step, 2)
                v.tensor_tensor(bias_rest[:, :, :], bias[:, :, :], bias_parts[:, :, :], ALU.subtract).then_inc(bias_step, 1)
                dve.wait_ge(bias_step, 3)
                middle, low, none = (slice(32 * q, 32 * q + 32) for q in (1, 2, 3))
                v.tensor_copy(bias_mid[low, :, :], bias_rest[low, :, :]).then_inc(bias_step, 1)
                v.tensor_copy(bias_parts[middle, :, :], bias_rest[middle, :, :])
                v.memset(bias_parts[none, :, :], 0.0)
                dve.wait_ge(bias_step, 4)
                v.tensor_tensor(bias_parts[low, :, :], bias_rest[low, :, :], bias_mid[low, :, :], ALU.subtract).then_inc(bias_ready, 1)

            def statistics(n, source, g, s):
                for t in range(T):
                    last = v.bn_stats(stats[n][s][:, t, :], source(t))
                last.then_inc(stats_done[n], 1)

            def mean_variance(n, g, s):
                wait(dve, norm_done[n], g - 1)
                wait(dve, stats_done[n], g + 1)
                dve.sem_inc(waits_taken, 1)
                for t in range(T):
                    last = v.bn_aggr(mean_var[n][s][:, t, :], stats[n][s][:, t, :])
                last.then_inc(mean_var_done[n], 1)

            def normalize(n, to, source, g, s):
                wait(dve, rstd_done[n], g + 1)
                for t in range(T):
                    last = v.tensor_scalar(to[s][:, t, :], source(t), mean_var[n][s][:, t, 0:1], rstd[n][s][:, t:t + 1],
                                           ALU.subtract, ALU.mult)
                last.then_inc(norm_done[n], 1)

            def stats0(g, s):
                dve.wait_ge(x_in[s], graphs_in(g, s))
                statistics("0", lambda t: graph(x_all, g * T + t, D), g, s)

            def stats1(g, s):
                wait(dve, swish1_done, g + 1)
                statistics("1", lambda t: s1[s][:, t, :], g, s)

            def stats2(g, s):
                wait(dve, swish2_done, g + 1)
                statistics("2", lambda t: s2[s][:, t, :], g, s)

            def statsf(g, s):
                wait(dve, mlp2_done, g + 1)
                statistics("f", lambda t: ps_mlp2[:, t * D:(t + 1) * D], g, s)

            def stats3(g, s):
                wait(dve, x2_ready, g + 1)
                statistics("3", lambda t: graph(x2_all, g * T + t, D), g, s)

            def mean0(g, s):
                mean_variance("0", g, s)

            def mean1(g, s):
                mean_variance("1", g, s)

            def mean2(g, s):
                mean_variance("2", g, s)

            def meanf(g, s):
                mean_variance("f", g, s)

            def mean3(g, s):
                mean_variance("3", g, s)

            def shift0(g, s):
                wait(dve, norm_done["0"], g - 1)
                wait(dve, rstd_done["0"], g + 1)
                v.scalar_tensor_tensor(shift[s][:, :], mean_var["0"][s][:, :, 0], -1.0, rstd["0"][s][:, :], ALU.mult, ALU.mult).then_inc(shift_done, 1)

            def norm3(g, s):
                wait(dve, transposed["3"], g - 1)
                normalize("3", xn3, lambda t: graph(x2_all, g * T + t, D), g, s)

            def normf(g, s):
                wait(dve, x2_ready, g - 1)
                wait(dve, rstd_done["f"], g + 1)
                for t in range(T):
                    last = v.scalar_tensor_tensor(lnf[s][:, t, :], ps_mlp2[:, t * D:(t + 1) * D], rstd["f"][s][:, t:t + 1], lnf_w,
                                                  ALU.mult, ALU.mult)
                last.then_inc(norm_done["f"], 1)

            def make_mask(g, s):
                dve.wait_ge(adj_in[s], graphs_in(g, s))
                wait(dve, prob_ready, g - 1)
                v.tensor_scalar(mask[s][:, :, :].rearrange("p t (s q) -> p t s q", s=T),
                                graph(adj_all, g, R).rearrange("p (t q s) -> p t s q", t=T, s=T),
                                0, MASKED, ALU.is_equal, ALU.mult).then_inc(mask_ready, 1)

            def softmax_input(g, s):
                wait(dve, scores_done, g + 1)
                wait(dve, mask_ready, g + 1)
                dve.sem_inc(waits_taken, 1)
                for t in range(T):
                    last = v.tensor_tensor_reduce(out=mask[s][:, t, :], in0=ps_scores[:, t * N:(t + 1) * N], in1=mask[s][:, t, :],
                                                  scale=-1.0, scalar=3.0e38, op0=ALU.add, op1=ALU.min,
                                                  accum_out=neg_max[s][:, t:t + 1])
                last.then_inc(softmax_in, 1)

            def inverse_sum(g, s):
                wait(dve, prob_ready, g + 1)
                v.reciprocal(inv_sum[s][:, :], prob_sum[s][:, :]).then_inc(inv_sum_ready, 1)

            def swish1(g, s):
                wait(dve, norm_done["1"], g - 1)
                wait(dve, tanh1_done, g + 1)
                v.scalar_tensor_tensor(s1[s][:, :, :], th1[s][:, :, :], 1.0, attn[s][:, :, :], ALU.add, ALU.mult).then_inc(swish1_done, 1)

            def swish2(g, s):
                wait(dve, norm_done["2"], g - 1)
                wait(dve, tanh2_done, g + 1)
                v.scalar_tensor_tensor(s2[s][:, :, :], th2[s][:, :, :], 1.0, tiles(ps_mlp1[:, 0:W]), ALU.add, ALU.mult).then_inc(swish2_done, 1)

            def messages(g, s):
                wait(dve, aggregated, g - 1)
                wait(dve, tanh3_done, g + 1)
                v.scalar_tensor_tensor(vals[s][:, :, :], th3[s][:, :, :], 1.0,
                                       ps_rel[:, :].rearrange("p (t a d) -> p t a d", t=T, a=2)[:, :, 0, :],
                                       ALU.add, ALU.mult).then_inc(vals_ready, 1)

            def add_messages(g, s):
                if not isinstance(g, int) or g >= SLOTS:
                    dve.wait_ge(result_out[s], results_out(g, s))
                wait(dve, aggregated, g + 1)
                v.scalar_tensor_tensor(result[s][:, :, :], tiles(ps_t2out[:, 0:W]), 0.0, tiles(graph(x2_all, g, W)),
                                       ALU.max, ALU.add).then_inc(result_ready, 1)

            def flag_others():
                dve.wait_ge(squares_summed, G)
                v.reduce_max(square_max[:, :], square_sums[:, :], axis=mybir.AxisListType.X).then_inc(square_max_ready, 1)
                dve.wait_ge(square_max_ready, 1)
                for c in range(2):
                    last = v.tensor_scalar(others_row[:, c:c + 1], square_max[:, :], R / 4 + 1, None, ALU.is_gt)
                last.then_inc(others_row_ready, 1)
                dve.wait_ge(others_counted, 1)
                v.tensor_scalar(others_flag[:, :], ps_scores[0:1, 0:2], 32.0, None, ALU.mult).then_inc(flag_ready, 1)

            def step(i, u):
                stage("normf", normf, i, u)
                stage("mean2", mean2, i, u)
                stage("softmax_input", softmax_input, i, u)
                stage("norm3", norm3, i, u)
                if first("make_mask", i):
                    prepare_mlp()
                stage("make_mask", make_mask, i, u)
                stage("stats0", stats0, i, u)
                stage("shift0", shift0, i, u)
                if first("swish1", i):
                    split_biases()
                stage("swish1", swish1, i, u)
                stage("mean0", mean0, i, u)
                stage("statsf", statsf, i, u)
                stage("stats1", stats1, i, u)
                stage("inverse_sum", inverse_sum, i, u)
                stage("meanf", meanf, i, u)
                stage("mean1", mean1, i, u)
                stage("stats3", stats3, i, u)
                stage("messages", messages, i, u)
                stage("mean3", mean3, i, u)
                stage("add_messages", add_messages, i, u)
                stage("swish2", swish2, i, u)
                stage("stats2", stats2, i, u)

            run(dve, step, STAGES["dve"])
            flag_others()

            def general():
                for s in range(SLOTS):
                    dve.wait_ge(result_out[s], 16 * (G // SLOTS))
                dve.wait_ge(rows_numbered, 1)
                v.memset(sums[:, :], 0.0)

                def clear_table(d, name, first):
                    v.memset(table[:, :, :], 0.0).then_inc(table_cleared, 1)

                def normalize_nodes(g, k, first):
                    v.tensor_scalar(s2[0][:, :, :], tiles(graph(x2_all, g, W)), 1.0, None, ALU.mult).then_inc(node_copied, 1)
                    dve.wait_ge(node_copied, k + 1)
                    for t in range(T):
                        last = v.bn_stats(stats["3"][0][:, t, :], s2[0][:, t, :])
                    last.then_inc(node_stats, 1)
                    taken(dve, node_stats, k + 1)
                    for t in range(T):
                        last = v.bn_aggr(mean_var["3"][0][:, t, :], stats["3"][0][:, t, :])
                    last.then_inc(node_mean_var, 1)
                    dve.wait_ge(node_rstd, k + 1)
                    for t in range(T):
                        last = v.tensor_scalar(xn3[0][:, t, :], s2[0][:, t, :], mean_var["3"][0][:, t, 0:1], rstd["3"][0][:, t:t + 1],
                                               ALU.subtract, ALU.mult)
                    last.then_inc(node_normalized, 1)
                    v.memset(counters[:, 0:1], 0.0)
                    v.memset(counters[:, 1:2], float(first)).then_inc(counters_set, 1)
                    taken(dve, counters_set, k + 1)

                def relation(g, n, rows_receive):
                    v.tensor_scalar(row_pick, row_number, counters[:, 0:1], None, ALU.is_equal).then_inc(row_picked, 1)
                    v.tensor_scalar(edges[0][:, :, :].rearrange("p t (s q) -> p t s q", s=T),
                                    graph(adj_all, g, R).rearrange("p (t q s) -> p t s q", t=T, s=T),
                                    counters[:, 1:2], None, ALU.is_equal).then_inc(edges_ready, 1)
                    dve.wait_ge(gates_tanh, n + 1)
                    v.scalar_tensor_tensor(vals[0][:, :, :], th3[0][:, :, :], 1.0,
                                           ps_rel[:, :].rearrange("p (t a d) -> p t a d", t=T, a=2)[:, :, 0, :],
                                           ALU.add, ALU.mult).then_inc(messages_ready, 1)
                    dve.wait_ge(edges_ready, n + 1)
                    v.tensor_scalar(counters[:, :], counters[:, :], 1.0, None, ALU.add)
                    dve.wait_ge(messages_summed, n + 1)
                    v.tensor_tensor(tiles(graph(sums, g, W)), tiles(ps_t2out[:, 0:W]), tiles(graph(sums, g, W)), ALU.add).then_inc(sum_added, 1)
                    taken(dve, sum_added, n + 1)

                def finish(d, g):
                    if d < len(PASSES) - 1:
                        return
                    v.tensor_scalar(s2[0][:, :, :], tiles(graph(sums, g, W)), 0.5, 0.0, ALU.mult, ALU.max).then_inc(sum_halved, 1)
                    dve.wait_ge(sum_halved, g + 1)
                    v.tensor_tensor(result[0][:, :, :], s2[0][:, :, :], tiles(graph(x2_all, g, W)), ALU.add).then_inc(general_ready, 1)
                    dve.wait_ge(general_out, (g + 1) * 16)

                over_passes(dve, clear_table, normalize_nodes, relation, finish)

            if_others(dve, general)

        @block.tensor
        def _(pe):
            mm, transpose = nc.tensor.matmul, nc.tensor.transpose
            def prepare():
                pe.wait_ge(qkv_weights_in, 16)
                mm(ps_mlp1[:, 0:D], Wq, Wk, start=True, stop=True).then_inc(qk_product, 1)
                pe.wait_ge(consts_done, 6)

            def center_w2():
                pe.wait_ge(weights_in, 16 * WEIGHT_LOADS)
                mm(ps_mlp2[:, 0:D], W2, centering[:, :], start=True, stop=True).then_inc(w2_centered, 1)
                pe.wait_ge(qk_ready, 1)

            def prepare_mlp():
                pe.wait_ge(mlp_scaled, 1)
                mm(ps_mlp2[:, 0:2 * D], centering[:, :], W12s[:, :, :].rearrange("p a d -> p (a d)"), start=True, stop=True)
                for a, through in enumerate((identity, centering)):
                    mm(ps_rel[:, a * D:(a + 1) * D], wide[:, 2 * a, :], W12T[:, a, :], start=True, stop=False)
                    last = mm(ps_rel[:, a * D:(a + 1) * D], wide[:, 2 * a + 1, :], through[:, :], start=False, stop=True)
                last.then_inc(mlp_centered, 1)
                mm(ps_mlp1[:, 0:D], Wl, WgT, start=True, stop=True).then_inc(rel_gate_product, 1)

            def prepared():
                pe.wait_ge(mlp_ready, 1)
                pe.wait_ge(rel_gate_ready, 1)
                pe.wait_ge(bias_ready, 1)

            def transpose_rows(bank, source, n):
                for t in range(T):
                    last = transpose(bank[:, t * P:(t + 1) * P], source[:, t, :], identity[:, :])
                last.then_inc(transposed[n], 1)

            def linear(bank, xT, weights, biases, done):
                width = weights.shape[1]
                mm(bank[:, 0:T * width], thirtysecond[:, :], biases, start=True, stop=False, skip_group_check=True)
                for t in range(T):
                    last = mm(bank[:, t * width:(t + 1) * width], xT[:, t * P:(t + 1) * P], weights, start=False, stop=True,
                              skip_group_check=True)
                last.then_inc(done, 1)

            def transpose_probs(g, s):
                wait(pe, attn_ready, g)
                wait(pe, prob_ready, g + 1)
                for c in range(T):
                    for t in range(T):
                        last = transpose(ps_attn[:, c * N + t * P:c * N + (t + 1) * P], prob[s][:, t, c * P:(c + 1) * P], identity[:, :])
                last.then_inc(probT_done, 1)

            def scores(g, s):
                wait(pe, softmax_in, g)
                wait(pe, qkv_ready, g + 1)
                for t in range(T):
                    last = mm(ps_scores[:, t * N:(t + 1) * N], qkv[s][:, t * P:(t + 1) * P], hT[s][:, :], start=True, stop=True)
                last.then_inc(scores_done, 1)

            def transpose0(g, s):
                wait(pe, qkv_ready, g)
                wait(pe, norm_done["0"], g + 1)
                transpose_rows(ps_qkv, xn0[s], "0")

            def transpose1(g, s):
                wait(pe, norm_done["1"], g + 1)
                wait(pe, h2T_ready, g - 4)
                transpose_rows(ps_t13, xn1[s], "1")

            def transpose2(g, s):
                wait(pe, norm_done["2"], g + 1)
                wait(pe, result_ready, g - 4)
                transpose_rows(ps_t2out, xn2[s], "2")

            def transpose3(g, s):
                wait(pe, norm_done["3"], g + 1)
                wait(pe, n1T_ready, g + 5)
                transpose_rows(ps_t13, xn3[s], "3")

            def attend(g, s):
                wait(pe, probT_ready, g + 1)
                for t in range(T):
                    for c in range(T):
                        last = mm(ps_attn[:, t * D:(t + 1) * D], probT[s][:, c, t * P:(t + 1) * P],
                                  qkv[s][:, N + c * D:N + (c + 1) * D], start=(c == 0), stop=(c == T - 1))
                last.then_inc(attn_done, 1)

            def project(g, s):
                wait(pe, hT_ready, g + 1)
                mm(ps_qkv[:, 0:N], QK[:, :], hT[s][:, :], start=True, stop=True)
                for t in range(T):
                    last = mm(ps_qkv[:, N + t * D:N + (t + 1) * D], hT[s][:, t * P:(t + 1) * P], WvT, start=True, stop=True)
                last.then_inc(qkv_done, 1)

            def mlp1(g, s):
                wait(pe, n1T_ready, g + 1)
                wait(pe, swish2_done, g)
                linear(ps_mlp1, n1T[s], W12[:, 0, :], bias_parts[:, 0:1, :].to_broadcast([P, T, D]), mlp1_done)

            def mlp2(g, s):
                wait(pe, n2T_ready, g + 1)
                wait(pe, norm_done["f"], g)
                linear(ps_mlp2, n2T[s], W12[:, 1, :], bias_parts[:, 1:2, :].to_broadcast([P, T, D]), mlp2_done)

            def relate(g, s):
                wait(pe, h2T_ready, g + 1)
                wait(pe, vals_ready, g)
                linear(ps_rel, h2T[s], relW[:, :, :].rearrange("p a d -> p (a d)"),
                       bias_parts[:, 2:4, :].rearrange("p a d -> p (a d)").unsqueeze(1).to_broadcast([P, T, 2 * D]), rel_done)

            def aggregate(g, s):
                wait(pe, vals_ready, g + 1)
                wait(pe, edges_selected, g + 1)
                wait(pe, result_ready, g)
                wait(pe, n2T_ready, g + 5)
                for t in range(T):
                    for c in range(T):
                        last = mm(ps_t2out[:, t * D:(t + 1) * D], edges[s][:, c, t * P:(t + 1) * P], vals[s][:, c, :],
                                  start=(c == 0), stop=(c == T - 1))
                last.then_inc(aggregated, 1)

            prepare()

            def step(i, u):
                if first("mlp1", i):
                    prepared()
                stage("transpose2", transpose2, i, u)
                if first("project", i):
                    center_w2()
                stage("project", project, i, u)
                stage("relate", relate, i, u)
                stage("mlp2", mlp2, i, u)
                stage("transpose1", transpose1, i, u)
                stage("aggregate", aggregate, i, u)
                stage("transpose_probs", transpose_probs, i, u)
                stage("mlp1", mlp1, i, u)
                stage("transpose0", transpose0, i, u)
                stage("transpose3", transpose3, i, u)
                stage("scores", scores, i, u)
                if first("scores", i):
                    prepare_mlp()
                stage("attend", attend, i, u)

            run(pe, step, STAGES["pe"])
            pe.wait_ge(others_row_ready, 1)
            mm(ps_scores[:, 0:2], thirtysecond[:, :], others_row[:, :], start=True, stop=True).then_inc(others_counted, 1)

            def general():
                def prepare(d, name, first):
                    pe.wait_ge(pass_weights_in, 16 * 4 * (d + 1))
                    transpose(ps_scores[:, 0:D], Wl, identity[:, :])
                    transpose(ps_scores[:, D:2 * D], Wg[:, :], identity[:, :]).then_inc(pass_transposed, 1)
                    pe.wait_ge(pass_copied, d + 1)
                    mm(ps_scores[:, 0:D], Wl, WgT, start=True, stop=True).then_inc(pass_gated, 1)
                    pe.wait_ge(pass_ready, d + 1)

                def transpose_nodes(g, k, first):
                    pe.wait_ge(node_normalized, k + 1)
                    for t in range(T):
                        last = transpose(ps_t13[:, t * P:(t + 1) * P], xn3[0][:, t, :], identity[:, :])
                    last.then_inc(node_transposed, 1)
                    taken(pe, node_ready, k + 1)

                def relation(g, n, rows_receive):
                    pe.wait_ge(row_picked, n + 1)
                    weights, biases = (a[:, :, :].rearrange("p a d -> p (a d)") for a in (relW, table))
                    for t in range(T):
                        half = ps_rel[:, t * 2 * D:(t + 1) * 2 * D]
                        mm(half, row_pick, biases, start=True, stop=False)
                        last = mm(half, h2T[0][:, t * P:(t + 1) * P], weights, start=False, stop=True)
                    last.then_inc(gates_done, 1)
                    ends = edges[0]
                    pe.wait_ge(edges_ready, n + 1)
                    if rows_receive:
                        for c in range(T):
                            for t in range(T):
                                last = transpose(ps_attn[:, c * N + t * P:c * N + (t + 1) * P], edges[0][:, t, c * P:(c + 1) * P], identity[:, :])
                        last.then_inc(edges_transposed, 1)
                        pe.wait_ge(edges_copied, n + 1)
                        ends = probT[0]
                    pe.wait_ge(messages_ready, n + 1)
                    for t in range(T):
                        for c in range(T):
                            last = mm(ps_t2out[:, t * D:(t + 1) * D], ends[:, c, t * P:(t + 1) * P], vals[0][:, c, :],
                                      start=(c == 0), stop=(c == T - 1))
                    last.then_inc(messages_summed, 1)

                over_passes(pe, prepare, transpose_nodes, relation)

            if_others(pe, general)


SQUARE = ("Wq", "Wk", "WvT", "W1T", "W2", "W_loopT", "Wg_loopT", "W_loop")
COLUMNS = ("ln1_b", "b1", "ln2_b", "b2", "ln1_w", "ln2_w")
ROWS = ("b_loop", "bg_loop", "lnf_w", "lnf_b")
WEIGHT_LOADS = 3


def graphs_in(g, s):
    return 16 * (g // SLOTS + 1) if isinstance(g, int) else (g - s) * (16 // SLOTS) + 16


def results_out(g, s):
    return 16 * (g // SLOTS) if isinstance(g, int) else (g - s) * (16 // SLOTS)


_INS = ["x", "adj", *(f"L1_gnn_{kind}_{name}" for kind in ("W", "Wg", "b", "bg") for name in ("fwd", "bwd", "loop"))]


def kernel(**inputs):
    import numpy as np
    import concourse.bacc as bacc
    from concourse.bass_utils import run_bass_kernel_spmd

    nc = bacc.Bacc("TRN2", target_bir_lowering=False, num_devices=1)
    arrays, io = {}, {}
    for name in _INS:
        a = np.ascontiguousarray(inputs[name])
        arrays[f"in_{name}"] = a
        io[name] = nc.dram_tensor(f"in_{name}", a.shape, mybir.dt.from_np(a.dtype), kind="ExternalInput").ap()
    layer = {name[7:]: inputs[name] for name in inputs if name[:3] in ("L0_", "L1_")}
    square = np.stack([np.asarray(layer[n[:-1]]).T if n[-1] == "T" else np.asarray(layer[n]) for n in SQUARE], axis=1)
    columns = np.stack([np.asarray(layer[n]) for n in COLUMNS], axis=1)
    rows = np.concatenate([np.asarray(layer[n]).reshape(-1) for n in ROWS])
    for name, a in (("square", square), ("columns", columns), ("rows", rows)):
        a = np.ascontiguousarray(a)
        arrays[f"in_{name}"] = a
        io[name] = nc.dram_tensor(f"in_{name}", a.shape, FP32, kind="ExternalInput").ap()
    out = nc.dram_tensor("out", arrays["in_x"].shape, FP32, kind="ExternalOutput").ap()
    graph_layers(nc, io, out)
    r = run_bass_kernel_spmd(nc, [arrays], core_ids=[0])
    return r.results[0]["out"]
```
